# Optimizing a Trainium2 kernel written in Bass

```python
import numpy as np
import jax
import jax.numpy as jnp

def _softmax(x, axis=-1):
    return jax.nn.softmax(x, axis=axis)

def _gelu(x):
    return jax.nn.gelu(x, approximate=True)

def _silu(x):
    return jax.nn.silu(x)

def _sigmoid(x):
    return jax.nn.sigmoid(x)

def _layernorm(x, axis=-1, eps=1e-05):
    m = jnp.mean(x, axis=axis, keepdims=True)
    v = jnp.var(x, axis=axis, keepdims=True)
    return (x - m) / jnp.sqrt(v + eps)

def _scatter_add(tgt, idx, src, axis=0):
    return tgt.at[idx].add(src)

def _segment_sum(src, seg, n):
    return jax.ops.segment_sum(src, seg, n)
kernel_name = 'mk_gnn_preln_d4_gnn_r32_7e4ca6'

def setup_inputs(seed: int=0):
    np.random.seed(seed)
    _w = jnp.asarray

    def _rec_inputs():
        import jax
        import jax.numpy as jnp
        _gk = jax.random.key(seed)
        x = -0.0002117 + 1 * jax.random.normal(jax.random.fold_in(_gk, 1), (3125, 256), jnp.float32)
        _s = jax.random.randint(jax.random.fold_in(_gk, 2), (25000,), 0, 3125, jnp.int32)
        _d = jax.random.randint(jax.random.fold_in(_gk, 3), (25000,), 0, 3125, jnp.int32)
        _loop = jnp.arange(3125, dtype=jnp.int32)
        src = jnp.concatenate([_s, _d, _loop])
        dst = jnp.concatenate([_d, _s, _loop])
        _o = jnp.argsort(dst, stable=True)
        src = src[_o]
        dst = dst[_o]
        edge_type_8 = jax.random.randint(jax.random.fold_in(_gk, 13), (53125,), 0, 8, jnp.int32)
        edge_weight = jax.random.uniform(jax.random.fold_in(_gk, 14), (53125,), jnp.float32, 0.0, 1)
        return (x, src, dst, edge_type_8, edge_weight)
    x, src, dst, edge_type_8, edge_weight = _rec_inputs()

    def _L0_gnn_setup():
        import jax, jax.numpy as jnp
        import numpy as np
        N = 3125
        E = 100000
        D_IN = 256
        D_OUT = 256
        EPS = 1e-12
        key = jax.random.key(seed)
        k1, k2, k3, k4, k5, k6 = jax.random.split(key, 6)
        x = jax.random.normal(k1, (N, D_IN), dtype=jnp.float32)
        edge_src = jax.random.randint(k2, (E,), 0, N, dtype=jnp.int32)
        edge_dst = jax.random.randint(k3, (E,), 0, N, dtype=jnp.int32)
        edge_w = jax.random.uniform(k4, (E,), dtype=jnp.float32)
        w_self = jax.random.normal(k5, (D_OUT, D_IN), dtype=jnp.float32) * 0.05
        w_neigh = jax.random.normal(k6, (D_OUT, D_IN), dtype=jnp.float32) * 0.05
        return {'x': x, 'edge_src': edge_src, 'edge_dst': edge_dst, 'edge_w': edge_w, 'w_self': w_self, 'w_neigh': w_neigh}
    _L0_gnn_all = _L0_gnn_setup()
    _L0_gnn_in = {k: v for k, v in _L0_gnn_all.items() if k in ('w_self', 'w_neigh')}
    del _L0_gnn_all

    def _L1_gnn_setup():
        import jax, jax.numpy as jnp
        import numpy as np
        NUM_NODES = 3125
        IN_CH = 256
        HIDDEN = 128
        OUT_CH = 256
        NUM_EDGES = 100000

        def gcn_conv(x, W, b, src, dst, num_nodes):
            h = x @ W
            loop = jnp.arange(num_nodes, dtype=src.dtype)
            s = jnp.concatenate([src, loop])
            d = jnp.concatenate([dst, loop])
            deg = jax.ops.segment_sum(jnp.ones_like(d, dtype=h.dtype), d, num_segments=num_nodes)
            dinv = jnp.where(deg > 0, jax.lax.rsqrt(deg), 0.0)
            norm = dinv[s] * dinv[d]
            msg = h[s] * norm[:, None]
            out = jax.ops.segment_sum(msg, d, num_segments=num_nodes)
            return out + b
        key = jax.random.key(seed)
        k1, k2, k3, k4 = jax.random.split(key, 4)
        edge_index = jax.random.randint(k1, (2, NUM_EDGES), 0, NUM_NODES, dtype=jnp.int64)
        node_features = jax.random.normal(k2, (NUM_NODES, IN_CH), dtype=jnp.float32)
        W1 = jax.random.normal(k3, (IN_CH, HIDDEN), dtype=jnp.float32) * (1.0 / np.sqrt(IN_CH))
        b1 = jnp.zeros((HIDDEN,), dtype=jnp.float32)
        W2 = jax.random.normal(k4, (HIDDEN, OUT_CH), dtype=jnp.float32) * (1.0 / np.sqrt(HIDDEN))
        b2 = jnp.zeros((OUT_CH,), dtype=jnp.float32)
        return {'node_features': node_features, 'W1': W1, 'b1': b1, 'W2': W2, 'b2': b2, 'edge_index': edge_index}
    _L1_gnn_all = _L1_gnn_setup()
    _L1_gnn_in = {k: v for k, v in _L1_gnn_all.items() if k in ('W1', 'b1', 'W2', 'b2')}
    del _L1_gnn_all

    def _L2_gnn_setup():
        import jax, jax.numpy as jnp
        import numpy as np
        N_NODES = 3125
        K_HOPS = 2
        ALPHA = 0.5

        def _gcn_norm(edge_index, edge_weight, num_nodes):
            loops = jnp.arange(num_nodes, dtype=edge_index.dtype)
            src = jnp.concatenate([edge_index[0], loops])
            dst = jnp.concatenate([edge_index[1], loops])
            w = jnp.concatenate([edge_weight, jnp.ones((num_nodes,), edge_weight.dtype)])
            deg = jax.ops.segment_sum(w, dst, num_segments=num_nodes)
            dinv = jnp.where(deg > 0, jax.lax.rsqrt(jnp.maximum(deg, 1e-12)), 0.0)
            norm = dinv[src] * w * dinv[dst]
            return (src, dst, norm)
        key = jax.random.key(seed)
        k1, k2, k3, k4, k5 = jax.random.split(key, 5)
        N, E, D_IN, D_OUT = (N_NODES, 100000, 256, 256)
        x = jax.random.normal(k1, (N, D_IN), dtype=jnp.float32)
        edge_index = jax.random.randint(k2, (2, E), 0, N, dtype=jnp.int64)
        edge_weight = jax.random.uniform(k3, (E,), dtype=jnp.float32)
        W = jax.random.normal(k4, (D_OUT, D_IN), dtype=jnp.float32) / np.sqrt(D_IN)
        b = jax.random.normal(k5, (D_OUT,), dtype=jnp.float32) * 0.01
        return {'x': x, 'edge_index': edge_index, 'edge_weight': edge_weight, 'W': W, 'b': b}
    _L2_gnn_all = _L2_gnn_setup()
    _L2_gnn_in = {k: v for k, v in _L2_gnn_all.items() if k in ('W', 'b')}
    del _L2_gnn_all

    def _L3_gnn_setup():
        import jax, jax.numpy as jnp
        import numpy as np
        N_NODES = 50000
        N_EDGES = 25000
        N_REL = 8
        DIM = 256

        def _rgcn_layer(x, W, b, src, dst, edge_type, num_nodes):
            xt = jnp.einsum('ni,rio->rno', x, W)
            msg = jax.nn.relu(xt[edge_type, src] + b)
            return jax.ops.segment_sum(msg, dst, num_segments=num_nodes)
        key = jax.random.key(seed)
        ks = jax.random.split(key, 6)
        x = jax.random.normal(ks[0], (N_NODES, DIM), dtype=jnp.float32)
        limit = float(np.sqrt(6.0 / (DIM + DIM)))
        W0 = jax.random.uniform(ks[1], (N_REL, DIM, DIM), dtype=jnp.float32, minval=-limit, maxval=limit)
        W1 = jax.random.uniform(ks[2], (N_REL, DIM, DIM), dtype=jnp.float32, minval=-limit, maxval=limit)
        b0 = jnp.zeros((DIM,), dtype=jnp.float32)
        b1 = jnp.zeros((DIM,), dtype=jnp.float32)
        edge_index = jax.random.randint(ks[3], (2, N_EDGES), 0, N_NODES, dtype=jnp.int64)
        edge_type = jax.random.randint(ks[4], (N_EDGES,), 0, N_REL, dtype=jnp.int64)
        return {'x': x, 'W0': W0, 'b0': b0, 'W1': W1, 'b1': b1, 'edge_index': edge_index, 'edge_type': edge_type}
    _L3_gnn_all = _L3_gnn_setup()
    _L3_gnn_in = {k: v for k, v in _L3_gnn_all.items() if k in ('W0', 'b0', 'W1', 'b1')}
    del _L3_gnn_all
    return {'x': x, 'src': src, 'dst': dst, 'edge_type_8': edge_type_8, 'edge_weight': edge_weight, 'L0_gnn_w_self': _L0_gnn_in['w_self'], 'L0_gnn_w_neigh': _L0_gnn_in['w_neigh'], 'L1_gnn_W1': _L1_gnn_in['W1'], 'L1_gnn_b1': _L1_gnn_in['b1'], 'L1_gnn_W2': _L1_gnn_in['W2'], 'L1_gnn_b2': _L1_gnn_in['b2'], 'L2_gnn_W': _L2_gnn_in['W'], 'L2_gnn_b': _L2_gnn_in['b'], 'L3_gnn_W0': _L3_gnn_in['W0'], 'L3_gnn_b0': _L3_gnn_in['b0'], 'L3_gnn_W1': _L3_gnn_in['W1'], 'L3_gnn_b1': _L3_gnn_in['b1']}

def reference(x, src, dst, edge_type_8, edge_weight, L0_gnn_w_self, L0_gnn_w_neigh, L1_gnn_W1, L1_gnn_b1, L1_gnn_W2, L1_gnn_b2, L2_gnn_W, L2_gnn_b, L3_gnn_W0, L3_gnn_b0, L3_gnn_W1, L3_gnn_b1):
    import jax
    import jax.numpy as jnp

    def _L0_gnn_ref(x, edge_src, edge_dst, edge_w, w_self, w_neigh):
        import jax, jax.numpy as jnp
        import numpy as np
        N = 3125
        E = 100000
        D_IN = 256
        D_OUT = 256
        EPS = 1e-12
        x_self = x @ w_self.T
        msgs = edge_w[:, None] * x[edge_src]
        x_neigh = jax.ops.segment_sum(msgs, edge_dst, num_segments=N)
        x_neigh = x_neigh @ w_neigh.T
        out = x_self + x_neigh
        norm = jnp.sqrt(jnp.sum(out * out, axis=1, keepdims=True))
        return out / jnp.maximum(norm, EPS)

    def _L1_gnn_ref(node_features, W1, b1, W2, b2, edge_index):
        import jax, jax.numpy as jnp
        import numpy as np
        NUM_NODES = 3125
        IN_CH = 256
        HIDDEN = 128
        OUT_CH = 256
        NUM_EDGES = 100000

        def gcn_conv(x, W, b, src, dst, num_nodes):
            h = x @ W
            loop = jnp.arange(num_nodes, dtype=src.dtype)
            s = jnp.concatenate([src, loop])
            d = jnp.concatenate([dst, loop])
            deg = jax.ops.segment_sum(jnp.ones_like(d, dtype=h.dtype), d, num_segments=num_nodes)
            dinv = jnp.where(deg > 0, jax.lax.rsqrt(deg), 0.0)
            norm = dinv[s] * dinv[d]
            msg = h[s] * norm[:, None]
            out = jax.ops.segment_sum(msg, d, num_segments=num_nodes)
            return out + b
        src, dst = (edge_index[0], edge_index[1])
        x = gcn_conv(node_features, W1, b1, src, dst, NUM_NODES)
        x = jax.nn.relu(x)
        x = gcn_conv(x, W2, b2, src, dst, NUM_NODES)
        return x

    def _L2_gnn_ref(x, edge_index, edge_weight, W, b):
        import jax, jax.numpy as jnp
        import numpy as np
        N_NODES = 3125
        K_HOPS = 2
        ALPHA = 0.5

        def _gcn_norm(edge_index, edge_weight, num_nodes):
            loops = jnp.arange(num_nodes, dtype=edge_index.dtype)
            src = jnp.concatenate([edge_index[0], loops])
            dst = jnp.concatenate([edge_index[1], loops])
            w = jnp.concatenate([edge_weight, jnp.ones((num_nodes,), edge_weight.dtype)])
            deg = jax.ops.segment_sum(w, dst, num_segments=num_nodes)
            dinv = jnp.where(deg > 0, jax.lax.rsqrt(jnp.maximum(deg, 1e-12)), 0.0)
            norm = dinv[src] * w * dinv[dst]
            return (src, dst, norm)
        N = x.shape[0]
        src, dst, norm = _gcn_norm(edge_index, edge_weight, N)
        h = x
        for _ in range(K_HOPS):
            msg = jax.ops.segment_sum(norm[:, None] * h[src], dst, num_segments=N)
            h = (1.0 - ALPHA) * msg + ALPHA * x
        h = jax.nn.relu(h)
        return h @ W.T + b

    def _L3_gnn_ref(x, W0, b0, W1, b1, edge_index, edge_type):
        import jax, jax.numpy as jnp
        import numpy as np
        N_NODES = 50000
        N_EDGES = 25000
        N_REL = 8
        DIM = 256

        def _rgcn_layer(x, W, b, src, dst, edge_type, num_nodes):
            xt = jnp.einsum('ni,rio->rno', x, W)
            msg = jax.nn.relu(xt[edge_type, src] + b)
            return jax.ops.segment_sum(msg, dst, num_segments=num_nodes)
        src, dst = (edge_index[0], edge_index[1])
        h = _rgcn_layer(x, W0, b0, src, dst, edge_type, x.shape[0])
        h = _rgcn_layer(h, W1, b1, src, dst, edge_type, x.shape[0])
        return h
    edge_index = jnp.stack([src, dst])
    h = jnp.maximum(_layernorm(x, axis=-1), 0.0)
    x = x + _L0_gnn_ref(h, src, dst, edge_weight, L0_gnn_w_self, L0_gnn_w_neigh)
    h = jnp.maximum(_layernorm(x, axis=-1), 0.0)
    x = x + _L1_gnn_ref(h, L1_gnn_W1, L1_gnn_b1, L1_gnn_W2, L1_gnn_b2, edge_index)
    h = jnp.maximum(_layernorm(x, axis=-1), 0.0)
    x = x + _L2_gnn_ref(h, edge_index, edge_weight, L2_gnn_W, L2_gnn_b)
    h = jnp.maximum(_layernorm(x, axis=-1), 0.0)
    x = x + _L3_gnn_ref(h, L3_gnn_W0, L3_gnn_b0, L3_gnn_W1, L3_gnn_b1, edge_index, edge_type_8)
    return x

_drawn_inputs = setup_inputs


def setup_inputs(seed=0):
    import zlib

    import numpy as np

    out = dict(_drawn_inputs(seed))
    spreads = {'L1_gnn_b1': (0.0, 0.463),
     'L1_gnn_b2': (0.0, 0.316),
     'L3_gnn_b0': (0.0, 0.1),
     'L3_gnn_b1': (0.0, 0.402)}
    factors = {'edge_weight': 64.0, 'L0_gnn_w_self': 64.0, 'L0_gnn_w_neigh': 17.918, 'L2_gnn_b': 31.362}
    for name, (base, spread) in spreads.items():
        noise = np.random.default_rng([zlib.crc32(name.encode()), seed]).standard_normal(out[name].shape)
        drawn = base * np.exp(spread * noise) if base else spread * noise
        out[name] = jnp.asarray(drawn.astype(out[name].dtype))
    for name, factor in factors.items():
        out[name] = (out[name] * factor).astype(out[name].dtype)
    return out
```

```python
from contextlib import ExitStack

import numpy as np

import concourse.bass as bass
from concourse import mybir

F32 = mybir.dt.float32
I32 = mybir.dt.int32
U32 = mybir.dt.uint32
ALU = mybir.AluOpType
ACT = mybir.ActivationFunctionType
AXX = mybir.AxisListType.X

P = 128
LN_EPS = 1e-5
NORM_EPS = 1e-12
DEG_EPS = 1e-12
PAD_DST = 4095.0


class Steps:

    def __init__(self, eng, sem, per, t):
        self.eng, self.sem, self.per, self.t, self.k = eng, sem, per, t, 0

    def __call__(self, ins):
        self.k += 1
        ins.then_inc(self.sem, 1)
        self.eng.wait_ge(self.sem, self.t * self.per + self.k)

    def close(self):
        assert self.k == self.per, (self.k, self.per)


def build_gnn(nc, x, src, dst, edge_type, edge_weight, w_self, w_neigh, gcn_w1, gcn_b1, gcn_w2,
              gcn_b2, hop_w, hop_b, rel_w0, rel_b0, rel_w1, rel_b1, out):
    N, D = x.shape
    E = src.shape[0]
    HID = gcn_w1.shape[1]
    REL = rel_w0.shape[0]
    TILES = -(-N // P)
    LAST = N - (TILES - 1) * P
    NPAD = TILES * P
    CHUNKS = -(-E // P)
    QUAD = 4
    QUADS = CHUNKS // QUAD
    VISITS = QUADS + TILES - 1
    KB = D // P
    BUCKETS = TILES + 1
    QP, QB = 104, 4
    GRING = 32
    GQ = GRING // QUAD
    STAGE = 16
    BLOCKS = CHUNKS // STAGE
    ROUNDS = CHUNKS // GRING
    SHIFT = 9
    TSHIFT = 7
    assert QP * QB == CHUNKS and CHUNKS % GRING == 0 and GRING == 2 * STAGE and BLOCKS % 2 == 0
    assert TILES % 2 == 1 and D == 256 and HID == P and 1 << SHIFT == QUAD * P and 1 << TSHIFT == P
    X_LOADS = -(-(TILES - 1) // 8) + 1
    TAIL = E - (CHUNKS - 1) * P

    PASSES = {"sage": (True, D), "gcn1": (False, HID), "gcn2": (False, HID), "hop1": (True, D),
              "hop2": (True, D), "rel1": (False, D), "rel2": (False, D)}
    NAMES = list(PASSES)

    with ExitStack() as ctx:
        def sb(name, shape, dt=F32):
            return ctx.enter_context(nc.sbuf_tensor(name, shape, dt))

        def psum(name, shape):
            return ctx.enter_context(nc.psum_tensor(name, shape, F32))

        def sem(name):
            return ctx.enter_context(nc.semaphore(name))

        def dram(name, shape):
            return nc.dram_tensor(name, shape, F32).ap()

        tables = {n: dram(f"table_{n}", (NPAD, PASSES[n][1])) for n in NAMES[:5]}
        tables["rel1"] = dram("table_rel1", (REL * NPAD, D))
        tables["rel2"] = dram("table_rel2", (REL * NPAD, D))
        sorted_dram = dram("edges_sorted", (CHUNKS * P, 4))

        x_sb = sb("x_sb", [P, TILES * D])
        h_sb = sb("h_sb", [P, TILES * D])
        t_sb = sb("t_sb", [P, TILES * D])
        gathered = sb("gathered", [P, GRING * D])
        onehot = sb("onehot", [P, QUAD * P])
        onehot1 = sb("onehot1", [P, QUAD * P])
        iota = sb("iota", [P, NPAD])
        edges = sb("edges", [P, CHUNKS, 4])
        one_w = sb("one_w", [P, CHUNKS, 2])
        idx_node = sb("idx_node", [P, CHUNKS], U32)
        idx_rel = sb("idx_rel", [P, CHUNKS], U32)
        stage_idx = sb("stage_idx", [P, 2, STAGE], U32)
        stage_rec = sb("stage_rec", [P, 2, STAGE * 4])
        bounds = sb("bounds", [P, TILES + 1], I32)
        dinv = sb("dinv", [P, TILES, 2])
        hdinv = sb("hdinv", [P, TILES])
        ident = sb("ident", [P, P])
        lower = sb("lower", [P, P])
        ones = sb("ones", [P, P])
        eps = sb("eps", [P, 1])
        wself_t = sb("wself_t", [P, KB, D])
        wneigh_t = sb("wneigh_t", [P, KB, D])
        hopw_t = sb("hopw_t", [P, KB, D])
        w1_sb = sb("w1_sb", [P, KB, HID])
        w2_sb = sb("w2_sb", [P, D])
        relw = sb("relw", [P, KB, REL, D])
        y_sb = sb("y_sb", [P, REL, D])
        b1_sb = sb("b1_sb", [P, HID])
        b2_sb = sb("b2_sb", [P, D])
        hopb_sb = sb("hopb_sb", [P, D])
        relb_sb = sb("relb_sb", [P, 2, D])
        post = sb("post", [P, D])
        post2 = sb("post2", [P, D])
        turned = sb("turned", [P, 2 * KB, P])
        small = sb("small", [P, 16])
        bnst = sb("bnst", [P, 6])
        post2n = sb("post2n", [P, D])

        flat_i = h_sb[0:QP, 0:3 * QB * P].bitcast(I32)
        flat_w = h_sb[0:QP, 1536:1536 + QB * P]
        flat_f = h_sb[0:QP, 2048:2048 + 4 * QB * P]
        flat_s = t_sb[0:QP, 0:QB * P * 4]
        wraw = t_sb[:, 2048:2048 + 6 * D]
        SC = 4096
        tile_f = t_sb[:, SC:SC + CHUNKS]
        mask = t_sb[:, SC + 416:SC + 416 + CHUNKS]
        pos = t_sb[:, SC + 832:SC + 832 + CHUNKS]
        tile_i = h_sb[:, SC:SC + CHUNKS].bitcast(I32)
        pos_u = h_sb[:, SC + 416:SC + 416 + CHUNKS].bitcast(U32)
        scan = [h_sb[:, SC + 832:SC + 832 + 256 + CHUNKS], h_sb[:, SC + 1504:SC + 1504 + 256 + CHUNKS]]
        tot = t_sb[:, 5400:5400 + BUCKETS]
        base = t_sb[:, 5440:5440 + BUCKETS]
        ends = [t_sb[:, 5480:5480 + 32 + BUCKETS], t_sb[:, 5540:5540 + 32 + BUCKETS]]
        ends_i = t_sb[:, 5600:5600 + BUCKETS].bitcast(I32)
        ends_f = t_sb[:, 5640:5640 + BUCKETS]

        agg = [psum("agg0", [P, 512]), psum("agg1", [P, 512])]
        turn_ps = psum("turn_ps", [P, 2 * KB, P])
        prod = psum("prod", [P, 512])
        y_ps = [psum("y0", [P, 2, D]), psum("y1", [P, 2, D])]


        s_x = sem("x_loaded")
        s_edge = sem("edges_loaded")
        s_w = sem("weights_loaded")
        s_wrel = [sem("rel_w0_loaded"), sem("rel_w1_loaded")]
        s_fill = sem("memory_filled")
        s_pad = sem("padding_ready")
        s_const = sem("constants_made")
        s_prep = sem("prep_dve_steps")
        s_flat = sem("flat_fields_ready")
        s_flat_t = sem("flat_fields_turned")
        s_edgef = sem("edge_fields_copied")
        s_tot = sem("bucket_totals_ready")
        s_totmm = sem("bucket_offsets_ready")
        s_pos = sem("positions_ready")
        s_stage = sem("stage_filled")
        s_total_steps = sem("total_steps")
        s_rank = sem("rank_steps")
        s_idx = sem("indices_ready")
        s_wt = sem("weight_turned")
        s_wtc = sem("weight_turned_copied")
        s_lnv = sem("first_norm_variance")
        s_lns = sem("first_norm_std")
        s_lnh = sem("first_norm_ready")
        s_ln = sem("first_norm_steps")
        s_srt = sem("sorted_reloaded")
        s_out = sem("out_stored")
        s_passed = [sem("pool_wait_passed"), sem("dve_wait_passed")]
        s_land = [sem(f"slot_landed{k}") for k in range(GRING)]

        S = {}
        for n in NAMES:
            for what in ("quad_landed", "quad_free", "onehot_ready", "pair_free", "agg_ready",
                         "agg_free", "table_ready", "table_stored", "dve_steps"):
                S[n, what] = sem(f"{n}_{what}")
        norm = ("var_ready", "std_ready")
        product = ("rows_ready", "rows_turned", "turned_copied", "product_ready")
        ys = ("y_ready", "y_added", "y_in_sbuf")
        for n, names in {"sage": product + norm + ("self_copied", "square_ready", "length_ready",
                                                   "degree_ready", "degree_root"),
                         "gcn2": product + norm, "hop2": product + norm + ys,
                         "rel1": product + ys}.items():
            for what in names:
                S[n, what] = sem(f"{n}_{what}")

        block = ctx.enter_context(nc.Block())

        def xt(t):
            return x_sb[:, bass.ds(t * D, D)]

        def ht(t):
            return h_sb[:, bass.ds(t * D, D)]

        def tt(t, w=D):
            return t_sb[:, bass.ds(t * D, w)]

        def over_tiles(eng, visits, rest):
            visits(0, 0)
            with eng.Fori(0, TILES // 2) as i:
                visits(i * 2 + 1, 1)
                rest(i * 2, 0)
                visits(i * 2 + 2, 0)
                rest(i * 2 + 1, 1)
            rest(TILES - 1, 0)

        @block.sync
        def _(sp):
            sp.wait_ge(s_pad, 1)
            full = (CHUNKS - QP) * P
            for k, a in enumerate((src, dst, edge_type, edge_weight)):
                d = flat_w if k == 3 else flat_i[:, k * QB * P:(k + 1) * QB * P]
                sp.dma_start(d[:, 0:(QB - 1) * P].rearrange("q (b e) -> q b e", e=P),
                             a[0:full].rearrange("(b q e) -> q b e", q=QP, e=P)).then_inc(s_edge, 16)
                sp.dma_start(d[0:QP - 1, (QB - 1) * P:QB * P],
                             a[full:full + (QP - 1) * P].rearrange("(q e) -> q e", e=P)).then_inc(s_edge, 16)
                sp.dma_start(d[QP - 1:QP, (QB - 1) * P:(QB - 1) * P + TAIL],
                             a[full + (QP - 1) * P:E].rearrange("(q e) -> q e", q=1)).then_inc(s_edge, 16)
            for lo in range(0, TILES - 1, 8):
                hi = min(lo + 8, TILES - 1)
                sp.dma_start(x_sb[:, lo * D:hi * D].rearrange("p (t d) -> p t d", d=D),
                             x[lo * P:hi * P].rearrange("(t p) d -> p t d", p=P)).then_inc(s_x, 16)
            sp.dma_start(x_sb[0:LAST, (TILES - 1) * D:TILES * D], x[(TILES - 1) * P:N]).then_inc(s_x, 16)
            for k, w in enumerate((w_self, w_neigh, hop_w)):
                sp.dma_start(wraw[:, k * KB * D:(k + 1) * KB * D].rearrange("p (m i) -> p m i", m=KB),
                             w.rearrange("(m p) i -> p m i", p=P)).then_inc(s_w, 16)
            sp.dma_start(w1_sb[:], gcn_w1.rearrange("(k p) o -> p k o", p=P)).then_inc(s_w, 16)
            sp.dma_start(w2_sb[:], gcn_w2).then_inc(s_w, 16)
            sp.dma_start(b1_sb[:], gcn_b1.partition_broadcast(P)).then_inc(s_w, 16)
            sp.dma_start(b2_sb[:], gcn_b2.partition_broadcast(P)).then_inc(s_w, 16)
            sp.dma_start(hopb_sb[:], hop_b.partition_broadcast(P)).then_inc(s_w, 16)

            def load_relations(w, b, s):
                for j in range(2):
                    sp.dma_start(relb_sb[:, j, :], b.partition_broadcast(P)).then_inc(s, 16)
                for k in range(KB):
                    sp.dma_start(relw[:, k, :, :], w[:, k * P:(k + 1) * P, :].rearrange("r p o -> p r o")
                                 ).then_inc(s, 16)

            load_relations(rel_w0, rel_b0, s_wrel[0])

            for k in range(GRING):
                sp.wait_ge(s_land[k], 16 * ROUNDS)
            for b in range(QB):
                sp.dma_start(flat_s[:, b * 4 * P:(b + 1) * 4 * P],
                             sorted_dram[b * QP * P:(b + 1) * QP * P].rearrange("(q e) f -> q (e f)", q=QP)
                             ).then_inc(s_srt, 16)

            for pi, n in enumerate(NAMES):
                if n == "rel1":
                    sp.wait_ge(S["rel1", "table_stored"], 16 * TILES)
                    load_relations(rel_w1, rel_b1, s_wrel[1])
                sp.sem_inc(S[n, "quad_landed"], QUAD)
                with sp.Fori(0, ROUNDS) as r:
                    for k in range(GRING):
                        sp.wait_ge(s_land[k], (r + (1 + pi * ROUNDS + ROUNDS)) * 16)
                        if k % QUAD == QUAD - 1:
                            sp.sem_inc(S[n, "quad_landed"], 1)
            sp.wait_ge(s_out, 16 * TILES)

        @block.gpsimd
        def _(pool):
            nc.gpsimd.memset(flat_i[:, 0:QB * P], 0).then_inc(s_fill, 1)
            nc.gpsimd.memset(flat_i[:, QB * P:2 * QB * P], int(PAD_DST)).then_inc(s_fill, 1)
            nc.gpsimd.memset(flat_i[:, 2 * QB * P:3 * QB * P], 0).then_inc(s_fill, 1)
            nc.gpsimd.memset(flat_w, 0.0).then_inc(s_fill, 1)
            nc.gpsimd.memset(x_sb[:, (TILES - 1) * D:TILES * D], 0.0).then_inc(s_fill, 1)
            pool.wait_ge(s_fill, 5)
            pool.sem_inc(s_pad, 1)
            nc.gpsimd.iota(iota[:], pattern=[[1, NPAD]], base=0, channel_multiplier=0,
                           allow_small_or_imprecise_dtypes=True).then_inc(s_const, 1)
            nc.gpsimd.memset(ident[:], 0.0).then_inc(s_fill, 1)
            nc.gpsimd.memset(lower[:], 0.0).then_inc(s_fill, 1)
            pool.wait_ge(s_fill, 7)
            nc.gpsimd.affine_select(out=ident[:], in_=ident[:], compare_op=ALU.not_equal, fill=1.0,
                                    base=0, pattern=[[-1, P]], channel_multiplier=1).then_inc(s_const, 1)
            nc.gpsimd.affine_select(out=lower[:], in_=lower[:], compare_op=ALU.is_ge, fill=1.0,
                                    base=0, pattern=[[-1, P]], channel_multiplier=1).then_inc(s_const, 1)
            nc.gpsimd.memset(ones[:], 1.0).then_inc(s_const, 1)
            nc.gpsimd.memset(eps[:], LN_EPS).then_inc(s_const, 1)

            pool.wait_ge(s_pos, 1)
            with pool.Fori(0, ROUNDS) as r:
                for h in range(2):
                    for k in range(STAGE):
                        pool.wait_ge(s_land[h * STAGE + k], r * 16)
                    c = r * GRING + h * STAGE
                    nc.gpsimd.tensor_copy(stage_idx[:, h, :], pos_u[:, bass.ds(c, STAGE)]).then_inc(s_stage, 1)
                    nc.gpsimd.tensor_copy(stage_rec[:, h, :].rearrange("p (c f) -> p c f", f=4),
                                          edges[:, bass.ds(c, STAGE), :]).then_inc(s_stage, 1)
                    pool.wait_ge(s_stage, r * 4 + (2 * h + 2))
                    pool.sem_inc(s_passed[0], 1)
                    for k in range(STAGE):
                        pool.indirect_dma_start(
                            sorted_dram, bass.IndirectOffsetOnAxis(ap=stage_idx[:, h, k:k + 1], axis=0),
                            stage_rec[:, h, k * 4:(k + 1) * 4], None).then_inc(s_land[h * STAGE + k], 16)

            pool.wait_ge(s_idx, 2)
            for pi, n in enumerate(NAMES):
                width = PASSES[n][1]
                index = idx_rel if n in ("rel1", "rel2") else idx_node
                pool.wait_ge(S[n, "table_stored"], 16 * TILES)
                with pool.Fori(0, ROUNDS) as r:
                    for h in range(2):
                        pool.wait_ge(S[n, "quad_landed"], r * GQ + h * QUAD)
                        nc.gpsimd.tensor_copy(stage_idx[:, h, :],
                                              index[:, bass.ds(r * GRING + h * STAGE, STAGE)]).then_inc(s_stage, 1)
                        pool.wait_ge(s_stage, r * 2 + (4 * ROUNDS + 2 * ROUNDS * pi + h + 1))
                        for k in range(STAGE):
                            slot = h * STAGE + k
                            if k % QUAD == 0:
                                pool.wait_ge(S[n, "quad_free"], r * GQ + (slot // QUAD + 1))
                                pool.sem_inc(s_passed[0], 1)
                            pool.indirect_dma_start(
                                gathered[:, slot * D:slot * D + width], None, tables[n],
                                bass.IndirectOffsetOnAxis(ap=stage_idx[:, h, k:k + 1], axis=0)
                            ).then_inc(s_land[slot], 16)

        def bounds_of(eng, t):
            first = eng.value_load(bounds[0:1, bass.ds(t, 1)], min_val=0, max_val=QUADS - 1)
            last = eng.value_load(bounds[0:1, bass.ds(t + 1, 1)], min_val=0, max_val=QUADS - 1)
            return first, last

        @block.tensor
        def _(pe):
            pe.wait_ge(s_const, 5)
            pe.wait_ge(s_w, 16 * 8)
            for k in range(3):
                if k >= 1:
                    pe.wait_ge(s_wtc, k)
                for m in range(KB):
                    for j in range(KB):
                        mm = pe.transpose(turn_ps[:, j * KB + m, :],
                                          wraw[:, (k * KB + m) * D + j * P:(k * KB + m) * D + (j + 1) * P], ident[:])
                mm.then_inc(s_wt, 1)

            def turn_edges(rows, first):
                for b in range(QB):
                    if first + b >= 2:
                        pe.wait_ge(s_edgef, first + b - 1)
                    for f in range(4):
                        mm = pe.transpose(y_ps[b % 2][0:P, f // 2, (f % 2) * P:(f % 2) * P + QP],
                                          rows(b, f), ident[0:QP, 0:QP])
                    mm.then_inc(s_flat_t, 1)

            pe.wait_ge(s_flat, 1)
            turn_edges(lambda b, f: flat_f[:, (f * QB + b) * P:(f * QB + b + 1) * P], 0)

            pe.wait_ge(s_tot, 1)
            pe.matmul(prod[:, 0:BUCKETS], ones[:], tot, start=True, stop=True)
            pe.matmul(prod[:, 64:64 + BUCKETS], lower[:], tot, start=True, stop=True).then_inc(s_totmm, 1)

            pe.wait_ge(s_srt, 16 * QB)
            turn_edges(lambda b, f: flat_s[:, b * 4 * P:(b + 1) * 4 * P].rearrange("q (e f) -> q f e", f=4)[:, f, :], QB)
            pe.wait_ge(s_idx, 4)

            def visits_of(n):
                weighted, width = PASSES[n]
                per = 2 if n == "sage" else 1

                def group(q, t, b, first):
                    u = q + t
                    pe.wait_ge(S[n, "quad_landed"], q + (QUAD + 1))
                    for k in range(QUAD):
                        pe.wait_ge(S[n, "onehot_ready"], u * (QUAD * per) + (k + 1) * per)
                        mm = pe.matmul(agg[b][:, 0:width], onehot[:, k * P:(k + 1) * P],
                                       gathered[:, bass.ds((q & (GQ - 1)) * (QUAD * D) + k * D, width)],
                                       start=first and k == 0, stop=True, skip_group_check=True)
                        if n == "sage":
                            mm = pe.matmul(agg[b][:, D:D + 2], onehot1[:, k * P:(k + 1) * P],
                                           one_w[:, bass.ds(q * QUAD + k, 1), :].rearrange("p c k -> p (c k)"),
                                           start=False, stop=True, skip_group_check=True)
                        if k % 2 == 1:
                            mm.then_inc(S[n, "pair_free"], 1)
                        elif k == 0 and not first:
                            mm.then_inc(S[n, "quad_free"], 1)

                def visits(t, b):
                    lo, hi = bounds_of(pe, t)
                    if not isinstance(t, int) or t >= 2:
                        pe.wait_ge(S[n, "agg_free"], t - 1)
                    group(lo, t, b, True)
                    with pe.If(lo < hi):
                        with pe.Fori(lo + 1, hi + 1) as q:
                            group(q, t, b, False)
                    pe.drain().then_inc(S[n, "agg_ready"], 1)
                return visits

            def turn(n, rows, t, j, per):
                pe.wait_ge(S[n, "rows_ready"], t * per + (j + 1))
                for k, r in enumerate(rows):
                    mm = pe.transpose(turn_ps[:, k, :], r, ident[:])
                mm.then_inc(S[n, "rows_turned"], 1)
                pe.wait_ge(S[n, "turned_copied"], t * per + (j + 1))

            def product(n, blocks, width):
                for k, w in enumerate(blocks):
                    mm = pe.matmul(prod[:, 0:width], turned[:, k, :], w,
                                   start=(k == 0), stop=(k == len(blocks) - 1))
                mm.then_inc(S[n, "product_ready"], 1)

            def relations(n, t):
                for g in range(REL // 2):
                    if g >= 2:
                        pe.wait_ge(S[n, "y_added"], t * (REL // 2) + (g - 1))
                    for k in range(KB):
                        mm = pe.matmul(y_ps[g % 2][:], turned[:, k, :], relw[:, k, 2 * g:2 * g + 2, :],
                                       start=(k == 0), stop=(k == KB - 1))
                    mm.then_inc(S[n, "y_ready"], 1)

            halves = [post[:, k * P:(k + 1) * P] for k in range(KB)]
            selfs = [post2[:, k * P:(k + 1) * P] for k in range(KB)]

            def sage_rest(t, b):
                pe.wait_ge(S["sage", "self_copied"], t + 1)
                turn("sage", halves + selfs, t, 0, 2)
                product("sage", [wneigh_t[:, k, :] for k in range(KB)] + [wself_t[:, k, :] for k in range(KB)], D)
                turn("sage", halves, t, 1, 2)
                product("sage", [w1_sb[:, k, :] for k in range(KB)], HID)

            def gcn2_rest(t, b):
                turn("gcn2", halves[0:1], t, 0, 1)
                product("gcn2", [w2_sb[:]], D)

            def hop2_rest(t, b):
                turn("hop2", halves, t, 0, 2)
                product("hop2", [hopw_t[:, k, :] for k in range(KB)], D)
                turn("hop2", halves, t, 1, 2)
                relations("hop2", t)

            def rel1_rest(t, b):
                turn("rel1", halves, t, 0, 1)
                relations("rel1", t)

            def nothing(t, b):
                pass

            rests = {"sage": sage_rest, "gcn1": nothing, "gcn2": gcn2_rest, "hop1": nothing,
                     "hop2": hop2_rest, "rel1": rel1_rest, "rel2": nothing}
            for n in NAMES:
                pe.sem_inc(S[n, "pair_free"], 2)
                pe.sem_inc(S[n, "quad_free"], GQ)
                if n == "hop2":
                    pe.wait_ge(s_wrel[0], 16 * (KB + 2))
                if n == "rel1":
                    pe.wait_ge(s_wrel[1], 16 * (KB + 2))
                over_tiles(pe, visits_of(n), rests[n])

        @block.scalar
        def _(act):
            for k, w in enumerate((wself_t, wneigh_t, hopw_t)):
                act.wait_ge(s_wt, k + 1)
                nc.scalar.copy(w[:].rearrange("p k o -> p (k o)"),
                               turn_ps[:].rearrange("p k o -> p (k o)")).then_inc(s_wtc, 1)

            with act.Fori(0, TILES) as t:
                act.wait_ge(s_lnv, t + 1)
                nc.scalar.activation(small[:, 2:3], small[:, 1:2], ACT.Sqrt, bias=eps[:]).then_inc(s_lns, 1)
                act.wait_ge(s_lnh, t + 1)
                act.dma_start(tables["sage"][bass.ds(t * P, P), :], ht(t)).then_inc(S["sage", "table_stored"], 16)

            def copy_turned(n, blocks, t, j, per):
                act.wait_ge(S[n, "rows_turned"], t * per + (j + 1))
                nc.scalar.copy(turned[:, 0:blocks, :].rearrange("p k o -> p (k o)"),
                               turn_ps[:, 0:blocks, :].rearrange("p k o -> p (k o)")
                               ).then_inc(S[n, "turned_copied"], 1)

            def root(n, t):
                act.wait_ge(S[n, "var_ready"], t + 1)
                nc.scalar.activation(small[:, 2:3], small[:, 1:2], ACT.Sqrt, bias=eps[:]
                                     ).then_inc(S[n, "std_ready"], 1)

            def store(n, to, t):
                act.wait_ge(S[n, "table_ready"], t + 1)
                act.dma_start(tables[to][bass.ds(t * P, P), :], tt(t, PASSES[to][1])
                              ).then_inc(S[to, "table_stored"], 16)

            def finish_relations(n, to, t):
                act.wait_ge(S[n, "y_added"], (t + 1) * (REL // 2))
                nc.scalar.activation(y_sb[:].rearrange("p r d -> p (r d)"), y_sb[:].rearrange("p r d -> p (r d)"),
                                     ACT.Relu).then_inc(S[n, "y_in_sbuf"], 1)
                act.wait_ge(S[n, "y_in_sbuf"], t + 1)
                act.dma_start(tables[to].rearrange("(r n) d -> n r d", r=REL)[bass.ds(t * P, P), :, :], y_sb[:]
                              ).then_inc(S[to, "table_stored"], 16)

            with act.Fori(0, TILES) as t:
                n = "sage"
                act.wait_ge(S[n, "rows_turned"], t * 2)
                nc.scalar.copy(post2[:], ht(t)).then_inc(S[n, "self_copied"], 1)
                act.wait_ge(S[n, "degree_ready"], t + 1)
                nc.scalar.activation(small[:, 10:12], small[:, 8:10], ACT.Sqrt).then_inc(S[n, "degree_root"], 1)
                copy_turned(n, 4, t, 0, 2)
                act.wait_ge(S[n, "product_ready"], t * 2 + 1)
                nc.scalar.activation(y_sb[:, 0, :], prod[:, 0:D], ACT.Square, accum_out=small[:, 4:5]
                                     ).then_inc(S[n, "square_ready"], 1)
                act.wait_ge(S[n, "square_ready"], t + 1)
                nc.scalar.activation(small[:, 5:6], small[:, 4:5], ACT.Sqrt).then_inc(S[n, "length_ready"], 1)
                root(n, t)
                copy_turned(n, 2, t, 1, 2)
                store(n, "gcn1", t)
            with act.Fori(0, TILES) as t:
                store("gcn1", "gcn2", t)
            with act.Fori(0, TILES) as t:
                copy_turned("gcn2", 1, t, 0, 1)
                root("gcn2", t)
                store("gcn2", "hop1", t)
            with act.Fori(0, TILES) as t:
                store("hop1", "hop2", t)
            with act.Fori(0, TILES) as t:
                copy_turned("hop2", 2, t, 0, 2)
                root("hop2", t)
                copy_turned("hop2", 2, t, 1, 2)
                finish_relations("hop2", "rel1", t)
            with act.Fori(0, TILES) as t:
                copy_turned("rel1", 2, t, 0, 1)
                finish_relations("rel1", "rel2", t)
            with act.Fori(0, TILES - 1) as t:
                act.wait_ge(S["rel2", "table_ready"], t + 1)
                act.dma_start(out[bass.ds(t * P, P), :], xt(t)).then_inc(s_out, 16)
            act.wait_ge(S["rel2", "table_ready"], TILES)
            act.dma_start(out[(TILES - 1) * P:N, :], x_sb[0:LAST, (TILES - 1) * D:TILES * D]).then_inc(s_out, 16)

        @block.vector
        def _(dve):
            prep = Steps(dve, s_prep, 0, 0)

            dve.wait_ge(s_edge, 16 * 12)
            for f, k in ((0, 0), (1, 1), (3, 2)):
                prep(nc.vector.tensor_copy(flat_f[:, f * QB * P:(f + 1) * QB * P],
                                           flat_i[:, k * QB * P:(k + 1) * QB * P]))
            nc.vector.tensor_copy(flat_f[:, 2 * QB * P:3 * QB * P], flat_w).then_inc(s_flat, 1)

            def copy_edges(first):
                for b in range(QB):
                    dve.wait_ge(s_flat_t, first + b + 1)
                    nc.vector.tensor_copy(
                        edges[:, b * QP:(b + 1) * QP, :],
                        y_ps[b % 2][:].rearrange("p a (g e) -> p e (a g)", g=2)[:, 0:QP, :]
                    ).then_inc(s_edgef, 1)
                dve.wait_ge(s_edgef, first + QB)

            copy_edges(0)

            dve.wait_ge(s_const, 5)
            prep(nc.vector.tensor_copy(tile_i, edges[:, :, 1]))
            prep(nc.vector.tensor_scalar(tile_i, tile_i, TSHIFT, None, ALU.logical_shift_right))
            prep(nc.vector.tensor_copy(tile_f, tile_i))
            prep(nc.vector.tensor_scalar(tile_f, tile_f, float(TILES), None, ALU.min))
            with dve.Fori(0, BUCKETS) as t:
                step = Steps(dve, s_total_steps, 2, t)
                step(nc.vector.tensor_scalar(mask, tile_f, iota[:, bass.ds(t, 1)], None, ALU.is_equal))
                step(nc.vector.tensor_reduce(tot[:, bass.ds(t, 1)], mask, AXX, ALU.add))
                step.close()
            dve.sem_inc(s_tot, 1)
            prep(nc.vector.memset(ends[0][:, 0:32], 0.0))
            prep(nc.vector.memset(ends[1][:, 0:32], 0.0))
            dve.wait_ge(s_totmm, 1)
            prep(nc.vector.tensor_copy(ends[0][:, 32:], prod[:, 0:BUCKETS]))
            prep(nc.vector.tensor_copy(ends_f, prod[:, 0:BUCKETS]))
            for j in range(5):
                a, b = ends[j % 2], ends[(j + 1) % 2]
                prep(nc.vector.tensor_tensor(b[:, 32:], a[:, 32:], a[:, 32 - (1 << j):-(1 << j)], ALU.add))
            end = ends[1][:, 32:]
            prep(nc.vector.tensor_tensor(base, end, ends_f, ALU.subtract))
            prep(nc.vector.scalar_tensor_tensor(base, base, -1.0, prod[:, 64:64 + BUCKETS], ALU.add, ALU.add))
            prep(nc.vector.tensor_copy(ends_i, end))
            prep(nc.vector.tensor_scalar(ends_i, ends_i, SHIFT, None, ALU.logical_shift_right))
            prep(nc.vector.memset(bounds[:], 0))
            prep(nc.vector.tensor_copy(bounds[:, 1:], ends_i[:, 0:TILES]))
            prep(nc.vector.memset(scan[0][:, 0:256], 0.0))
            prep(nc.vector.memset(scan[1][:, 0:256], 0.0))
            prep(nc.vector.memset(pos, 0.0))
            with dve.Fori(0, BUCKETS) as t:
                step = Steps(dve, s_rank, 13, t)
                step(nc.vector.tensor_scalar(scan[0][:, 256:], tile_f, iota[:, bass.ds(t, 1)], None, ALU.is_equal))
                step(nc.vector.tensor_copy(mask, scan[0][:, 256:]))
                for j in range(9):
                    a, b = scan[j % 2], scan[(j + 1) % 2]
                    step(nc.vector.tensor_tensor(b[:, 256:], a[:, 256:], a[:, 256 - (1 << j):-(1 << j)], ALU.add))
                step(nc.vector.scalar_tensor_tensor(mask, scan[1][:, 256:], base[:, bass.ds(t, 1)], mask,
                                                    ALU.add, ALU.mult))
                step(nc.vector.tensor_tensor(pos, pos, mask, ALU.add))
                step.close()
            prep(nc.vector.tensor_copy(pos_u, pos))
            dve.sem_inc(s_pos, 1)

            copy_edges(QB)
            nc.vector.tensor_copy(idx_node[:], edges[:, :, 0]).then_inc(s_idx, 1)
            nc.vector.scalar_tensor_tensor(idx_rel[:], edges[:, :, 3], float(NPAD), edges[:, :, 0],
                                           ALU.mult, ALU.add).then_inc(s_idx, 1)
            nc.vector.memset(one_w[:, :, 0], 1.0).then_inc(s_idx, 1)
            nc.vector.tensor_copy(one_w[:, :, 1], edges[:, :, 2]).then_inc(s_idx, 1)
            dve.wait_ge(s_idx, 4)

            def norm(step, rows, to, std):
                dve.sem_inc(s_passed[1], 1)
                step(nc.vector.bn_stats(bnst[:], rows))
                dve.sem_inc(s_passed[1], 1)
                nc.vector.bn_aggr(small[:, 0:2], bnst[:]).then_inc(std[0], 1)
                dve.wait_ge(std[1], step.t + 1)
                step(nc.vector.reciprocal(small[:, 3:4], small[:, 2:3]))
                step(nc.vector.tensor_scalar(post2n[:], rows, small[:, 0:1], 0.0, ALU.subtract, ALU.max))
                step(nc.vector.tensor_scalar(to, post2n[:], small[:, 3:4], None, ALU.mult))

            dve.wait_ge(s_x, 16 * X_LOADS)
            dve.wait_ge(s_wtc, 3)
            with dve.Fori(0, TILES) as t:
                step = Steps(dve, s_ln, 4, t)
                norm(step, xt(t), ht(t), (s_lnv, s_lns))
                dve.sem_inc(s_lnh, 1)
                step.close()

            def visits_of(n):
                weighted = PASSES[n][0]

                def visits(t, b):
                    lo, hi = bounds_of(dve, t)
                    with dve.Fori(lo, hi + 1) as q:
                        u = q + t
                        for k in range(QUAD):
                            if k % 2 == 0:
                                dve.wait_ge(S[n, "pair_free"], u * 2 + (k // 2 + 1))
                            edge = edges[:, bass.ds(q * QUAD + k, 1), :].rearrange("p c f -> p (c f)")
                            places = iota[:, bass.ds(t * P, P)]
                            to = onehot[:, k * P:(k + 1) * P]
                            if n == "sage":
                                nc.vector.tensor_scalar(onehot1[:, k * P:(k + 1) * P], places, edge[:, 1:2], None,
                                                        ALU.is_equal).then_inc(S[n, "onehot_ready"], 1)
                            if weighted:
                                ins = nc.vector.tensor_scalar(to, places, edge[:, 1:2], edge[:, 2:3],
                                                              ALU.is_equal, ALU.mult)
                            else:
                                ins = nc.vector.tensor_scalar(to, places, edge[:, 1:2], None, ALU.is_equal)
                            ins.then_inc(S[n, "onehot_ready"], 1)
                return visits

            def d(t, k):
                return dinv[:, bass.ds(t, 1), k:k + 1].rearrange("p a b -> p (a b)")

            def half_d(t):
                return hdinv[:, bass.ds(t, 1)]

            def rows_ready(n):
                dve.sem_inc(S[n, "rows_ready"], 1)

            def relations(n, t):
                dve.wait_ge(S[{"hop2": "rel1", "rel1": "rel2"}[n], "table_stored"], t * 16)
                for g in range(REL // 2):
                    dve.wait_ge(S[n, "y_ready"], t * (REL // 2) + (g + 1))
                    nc.vector.tensor_tensor(y_sb[:, 2 * g:2 * g + 2, :], y_ps[g % 2][:], relb_sb[:], ALU.add
                                            ).then_inc(S[n, "y_added"], 1)

            def sage_rest(t, b):
                n = "sage"
                step = Steps(dve, S[n, "dve_steps"], 14, t)
                dve.wait_ge(S[n, "agg_ready"], t + 1)
                step(nc.vector.tensor_copy(post[:], agg[b][:, 0:D]))
                rows_ready(n)
                step(nc.vector.tensor_scalar(small[:, 6:8], agg[b][:, D:D + 2], 1.0, None, ALU.add))
                dve.sem_inc(S[n, "agg_free"], 1)
                step(nc.vector.tensor_scalar(small[:, 8:10], small[:, 6:8], DEG_EPS, None, ALU.max))
                dve.sem_inc(S[n, "degree_ready"], 1)
                dve.wait_ge(S[n, "degree_root"], t + 1)
                step(nc.vector.reciprocal(small[:, 12:14], small[:, 10:12]))
                dt_ = dinv[:, bass.ds(t, 1), :].rearrange("p a b -> p (a b)")
                step(nc.vector.scalar_tensor_tensor(dt_, small[:, 6:8], 0.0, small[:, 12:14], ALU.is_gt, ALU.mult))
                step(nc.vector.tensor_scalar(half_d(t), d(t, 1), 0.5, None, ALU.mult))
                dve.wait_ge(S[n, "length_ready"], t + 1)
                step(nc.vector.tensor_scalar(small[:, 4:5], small[:, 5:6], NORM_EPS, None, ALU.max))
                step(nc.vector.reciprocal(small[:, 5:6], small[:, 4:5]))
                step(nc.vector.scalar_tensor_tensor(xt(t), prod[:, 0:D], small[:, 5:6], xt(t), ALU.mult, ALU.add))
                norm(step, xt(t), post[:], (S[n, "var_ready"], S[n, "std_ready"]))
                rows_ready(n)
                dve.wait_ge(S[n, "product_ready"], t * 2 + 2)
                step(nc.vector.tensor_scalar(tt(t, HID), prod[:, 0:HID], d(t, 0), None, ALU.mult))
                dve.sem_inc(S[n, "table_ready"], 1)
                step.close()

            def gcn1_rest(t, b):
                n = "gcn1"
                step = Steps(dve, S[n, "dve_steps"], 4, t)
                dve.wait_ge(S[n, "agg_ready"], t + 1)
                step(nc.vector.tensor_tensor(post[:, 0:HID], agg[b][:, 0:HID], tt(t, HID), ALU.add))
                dve.sem_inc(S[n, "agg_free"], 1)
                step(nc.vector.tensor_scalar(post[:, 0:HID], post[:, 0:HID], d(t, 0), None, ALU.mult))
                step(nc.vector.tensor_tensor(post[:, 0:HID], post[:, 0:HID], b1_sb[:], ALU.add))
                step(nc.vector.tensor_scalar(tt(t, HID), post[:, 0:HID], 0.0, d(t, 0), ALU.max, ALU.mult))
                dve.sem_inc(S[n, "table_ready"], 1)
                step.close()

            def gcn2_rest(t, b):
                n = "gcn2"
                step = Steps(dve, S[n, "dve_steps"], 9, t)
                dve.wait_ge(S[n, "agg_ready"], t + 1)
                step(nc.vector.tensor_tensor(post[:, 0:HID], agg[b][:, 0:HID], tt(t, HID), ALU.add))
                dve.sem_inc(S[n, "agg_free"], 1)
                step(nc.vector.tensor_scalar(post[:, 0:HID], post[:, 0:HID], d(t, 0), None, ALU.mult))
                rows_ready(n)
                step(nc.vector.tensor_tensor(xt(t), xt(t), b2_sb[:], ALU.add))
                dve.wait_ge(S[n, "product_ready"], t + 1)
                step(nc.vector.tensor_tensor(xt(t), prod[:, 0:D], xt(t), ALU.add))
                norm(step, xt(t), ht(t), (S[n, "var_ready"], S[n, "std_ready"]))
                step(nc.vector.tensor_scalar(tt(t), ht(t), d(t, 1), None, ALU.mult))
                dve.sem_inc(S[n, "table_ready"], 1)
                step.close()

            def hop(step, n, t, b):
                dve.wait_ge(S[n, "agg_ready"], t + 1)
                step(nc.vector.tensor_tensor(post[:], agg[b][:, 0:D], tt(t), ALU.add))
                dve.sem_inc(S[n, "agg_free"], 1)
                if n == "hop1":
                    step(nc.vector.tensor_scalar(ht(t), ht(t), 0.5, None, ALU.mult))
                step(nc.vector.scalar_tensor_tensor(post[:], post[:], half_d(t), ht(t), ALU.mult, ALU.add))

            def hop1_rest(t, b):
                step = Steps(dve, S["hop1", "dve_steps"], 4, t)
                hop(step, "hop1", t, b)
                step(nc.vector.tensor_scalar(tt(t), post[:], d(t, 1), None, ALU.mult))
                dve.sem_inc(S["hop1", "table_ready"], 1)
                step.close()

            def hop2_rest(t, b):
                n = "hop2"
                step = Steps(dve, S[n, "dve_steps"], 9, t)
                hop(step, n, t, b)
                step(nc.vector.tensor_scalar(post[:], post[:], 0.0, None, ALU.max))
                rows_ready(n)
                step(nc.vector.tensor_tensor(xt(t), xt(t), hopb_sb[:], ALU.add))
                dve.wait_ge(S[n, "product_ready"], t + 1)
                step(nc.vector.tensor_tensor(xt(t), prod[:, 0:D], xt(t), ALU.add))
                norm(step, xt(t), post[:], (S[n, "var_ready"], S[n, "std_ready"]))
                rows_ready(n)
                relations(n, t)
                step.close()

            def rel1_rest(t, b):
                n = "rel1"
                step = Steps(dve, S[n, "dve_steps"], 1, t)
                dve.wait_ge(S[n, "agg_ready"], t + 1)
                step(nc.vector.tensor_copy(post[:], agg[b][:, 0:D]))
                dve.sem_inc(S[n, "agg_free"], 1)
                rows_ready(n)
                relations(n, t)
                step.close()

            def rel2_rest(t, b):
                n = "rel2"
                dve.wait_ge(S[n, "agg_ready"], t + 1)
                step = Steps(dve, S[n, "dve_steps"], 1, t)
                step(nc.vector.tensor_tensor(xt(t), agg[b][:, 0:D], xt(t), ALU.add))
                dve.sem_inc(S[n, "agg_free"], 1)
                dve.sem_inc(S[n, "table_ready"], 1)
                step.close()

            rests = {"sage": sage_rest, "gcn1": gcn1_rest, "gcn2": gcn2_rest, "hop1": hop1_rest,
                     "hop2": hop2_rest, "rel1": rel1_rest, "rel2": rel2_rest}
            for n in NAMES:
                if n == "sage":
                    dve.wait_ge(s_w, 16 * 8)
                if n == "hop2":
                    dve.wait_ge(s_wrel[0], 16 * (KB + 2))
                if n == "rel1":
                    dve.wait_ge(s_wrel[1], 16 * (KB + 2))
                over_tiles(dve, visits_of(n), rests[n])


_INS = ["x", "src", "dst", "edge_type_8", "edge_weight", "L0_gnn_w_self", "L0_gnn_w_neigh", "L1_gnn_W1",
        "L1_gnn_b1", "L1_gnn_W2", "L1_gnn_b2", "L2_gnn_W", "L2_gnn_b", "L3_gnn_W0", "L3_gnn_b0",
        "L3_gnn_W1", "L3_gnn_b1"]


def kernel(**inputs):
    import concourse.bacc as bacc
    from concourse.bass_utils import run_bass_kernel_spmd

    nc = bacc.Bacc("TRN2", target_bir_lowering=False, num_devices=1)
    arrays, args = {}, []
    for name in _INS:
        a = np.ascontiguousarray(inputs[name])
        arrays[f"in_{name}"] = a
        args.append(nc.dram_tensor(f"in_{name}", a.shape, mybir.dt.from_np(a.dtype), kind="ExternalInput").ap())
    shape = inputs["x"].shape
    args.append(nc.dram_tensor("out_x", shape, F32, kind="ExternalOutput").ap())
    build_gnn(nc, *args)
    result = run_bass_kernel_spmd(nc, [arrays], core_ids=[0])
    return result.results[0]["out_x"]
```

```python
from contextlib import ExitStack

import numpy as np

import concourse.bass as bass
from concourse import mybir

F32 = mybir.dt.float32
BF16 = mybir.dt.bfloat16
I32 = mybir.dt.int32
U32 = mybir.dt.uint32
ALU = mybir.AluOpType
ACT = mybir.ActivationFunctionType
AXX = mybir.AxisListType.X

P = 128
LN_EPS = 1e-5
NORM_EPS = 1e-12
DEG_EPS = 1e-12
PAD_DST = 4095.0


class Steps:

    def __init__(self, eng, sem, per, t):
        self.eng, self.sem, self.per, self.t, self.k = eng, sem, per, t, 0

    def __call__(self, ins):
        self.k += 1
        ins.then_inc(self.sem, 1)
        self.eng.wait_ge(self.sem, self.t * self.per + self.k)

    def close(self):
        assert self.k == self.per, (self.k, self.per)


def build_gnn(nc, x, src, dst, edge_type, edge_weight, w_self, w_neigh, gcn_w1, gcn_b1, gcn_w2,
              gcn_b2, hop_w, hop_b, rel_w0, rel_b0, rel_w1, rel_b1, out):
    N, D = x.shape
    E = src.shape[0]
    HID = gcn_w1.shape[1]
    REL = rel_w0.shape[0]
    TILES = -(-N // P)
    LAST = N - (TILES - 1) * P
    NPAD = TILES * P
    CHUNKS = -(-E // P)
    QUAD = 4
    QUADS = CHUNKS // QUAD
    VISITS = QUADS + TILES - 1
    KB = D // P
    BUCKETS = TILES + 1
    QP, QB = 104, 4
    GRING = 32
    GQ = GRING // QUAD
    STAGE = 16
    BLOCKS = CHUNKS // STAGE
    AHEAD = QUAD + 1
    GROUP = 5
    ROUNDS = CHUNKS // GRING
    SHIFT = 9
    TSHIFT = 7
    assert QP * QB == CHUNKS and CHUNKS % GRING == 0 and GRING == 2 * STAGE
    assert TILES % GROUP == 0 and D == 256 and HID == P and 1 << SHIFT == QUAD * P and 1 << TSHIFT == P
    X_LOADS = -(-(TILES - 1) // 8) + 1
    TAIL = E - (CHUNKS - 1) * P

    PASSES = {"sage": (True, D), "gcn1": (False, HID), "gcn2": (False, HID), "hop1": (True, D),
              "hop2": (True, D), "rel1": (False, D), "rel2": (False, D)}
    NAMES = list(PASSES)

    with ExitStack() as ctx:
        def sb(name, shape, dt=F32):
            return ctx.enter_context(nc.sbuf_tensor(name, shape, dt))

        def psum(name, shape):
            return ctx.enter_context(nc.psum_tensor(name, shape, F32))

        def sem(name):
            return ctx.enter_context(nc.semaphore(name))

        def dram(name, shape):
            return nc.dram_tensor(name, shape, F32).ap()

        tables = {n: dram(f"table_{n}", (NPAD, PASSES[n][1])) for n in NAMES[:5]}
        tables["rel1"] = dram("table_rel1", (REL * NPAD, D))
        tables["rel2"] = dram("table_rel2", (REL * NPAD, D))
        sorted_dram = dram("edges_sorted", (CHUNKS * P, 4))

        x_sb = sb("x_sb", [P, TILES * D])
        h_sb = sb("h_sb", [P, TILES * D])
        t_sb = sb("t_sb", [P, TILES * D])
        gathered = sb("gathered", [P, GRING * D])
        onehot = sb("onehot", [P, QUAD * P])
        onehot1 = sb("onehot1", [P, QUAD * P], BF16)
        iota = sb("iota", [P, NPAD])
        edges = sb("edges", [P, CHUNKS, 4])
        one_w = sb("one_w", [P, CHUNKS, 4], BF16)
        idx_node = sb("idx_node", [P, CHUNKS], U32)
        idx_rel = sb("idx_rel", [P, CHUNKS], U32)
        stage_idx = sb("stage_idx", [P, 2, STAGE], U32)
        stage_rec = sb("stage_rec", [P, STAGE * 4])
        bounds = sb("bounds", [P, TILES + 1], I32)
        dinv = sb("dinv", [P, TILES, 2])
        hdinv = sb("hdinv", [P, TILES])
        ident = sb("ident", [P, P])
        lower = sb("lower", [P, P])
        ones = sb("ones", [P, P])
        eps = sb("eps", [P, 1])
        wself_t = sb("wself_t", [P, KB, D])
        wneigh_t = sb("wneigh_t", [P, KB, D])
        hopw_t = sb("hopw_t", [P, KB, D])
        w1_sb = sb("w1_sb", [P, KB, HID])
        w2_sb = sb("w2_sb", [P, D])
        relw = sb("relw", [P, KB, REL, D])
        y_sb = sb("y_sb", [P, REL, D])
        b1_sb = sb("b1_sb", [P, HID])
        b2_sb = sb("b2_sb", [P, D])
        hopb_sb = sb("hopb_sb", [P, D])
        relb_sb = sb("relb_sb", [P, 2, D])
        post = sb("post", [P, D])
        post2 = sb("post2", [P, D])
        turned = sb("turned", [P, 2 * KB, P])
        normed = sb("normed", [P, D])
        normed_t = sb("normed_t", [P, KB, P])
        small = sb("small", [P, 16])
        bnst = sb("bnst", [P, 6])
        bn_all = sb("bn_all", [P, TILES, 6])
        mv_all = sb("mv_all", [P, TILES, 2])
        rstd_all = sb("rstd_all", [P, TILES])
        flag = sb("flag", [P, 1], I32)
        post2n = sb("post2n", [P, D])

        F = QB * P
        flat_i = gathered[0:QP, 0:3 * F].bitcast(I32)
        flat_w = gathered[0:QP, 3 * F:4 * F]
        flat_next = gathered[0:QP, 4 * F:5 * F].bitcast(I32)
        flat_f = gathered[0:QP, 5 * F:9 * F]
        flat_s = gathered[0:QP, 9 * F:13 * F]
        drop = gathered[0:QP, 13 * F:14 * F]
        free = [0]

        def scratch(n):
            free[0] += n
            assert free[0] <= TILES * D
            return t_sb[:, free[0] - n:free[0]]

        wraw = scratch(3 * KB * D)
        tile_f, mask, pos, rest_w, rest_w2 = (scratch(CHUNKS) for _ in range(5))
        tile_i = scratch(CHUNKS).bitcast(I32)
        pos_u = scratch(CHUNKS).bitcast(U32)
        scan = [scratch(256 + CHUNKS) for _ in range(2)]
        tot, base, totals = (scratch(32)[:, 0:BUCKETS] for _ in range(3))
        ends = [scratch(32 + BUCKETS) for _ in range(2)]
        ends_i = scratch(32)[:, 0:BUCKETS].bitcast(I32)
        drops = scratch(2)

        agg = [psum("agg0", [P, 512]), psum("agg1", [P, 512])]
        turn_ps = psum("turn_ps", [P, 2 * KB, P])
        prod = psum("prod", [P, 512])
        prod2 = psum("prod2", [P, 512])
        y_ps = [psum("y0", [P, 2, D]), psum("y1", [P, 2, D])]


        s_x = sem("x_loaded")
        s_edge = sem("edges_loaded")
        s_w = sem("weights_loaded")
        s_wrel = [sem("rel_w0_loaded"), sem("rel_w1_loaded")]
        s_fill = sem("memory_filled")
        s_pad = sem("padding_ready")
        s_const = sem("constants_made")
        s_prep = sem("prep_dve_steps")
        s_flat = sem("flat_fields_ready")
        s_flat_t = sem("flat_fields_turned")
        s_edgef = sem("edge_fields_copied")
        s_tot = sem("bucket_totals_ready")
        s_totmm = sem("bucket_offsets_ready")
        s_pos = sem("positions_ready")
        s_stage = sem("stage_filled")
        s_total_steps = sem("total_steps")
        s_rank = sem("rank_steps")
        s_idx = sem("indices_ready")
        s_wt = sem("weight_turned")
        s_wtc = sem("weight_turned_copied")
        s_bn = sem("first_norm_stats")
        s_mv = sem("first_norm_variances")
        s_std = sem("first_norm_roots")
        s_rstd = sem("first_norm_scales")
        s_shift = sem("first_norm_shifted")
        s_scaled = sem("first_norm_scaled")
        s_drops = sem("drops_counted")
        s_dropmm = sem("drops_summed")
        s_flag = sem("flag_ready")
        s_scat = sem("records_scattered")
        s_scat_stage = sem("scatter_stage_filled")
        s_sort_prep = sem("sort_prep_steps")
        s_order_prep = sem("order_prep_steps")
        s_sort = sem("sort_steps")
        s_tot2 = sem("bucket_totals_in_order")
        s_totmm2 = sem("bucket_totals_summed")
        s_bounds = sem("bounds_ready")
        s_total_steps2 = sem("total_steps_in_order")
        s_srt = sem("sorted_reloaded")
        s_out = sem("out_stored")
        s_passed = [sem("pool_wait_passed"), sem("dve_wait_passed")]
        s_land = [sem(f"place_landed{k}") for k in range(GQ)]

        quad_landed = sem("quad_landed")
        quad_free = sem("quad_free")
        onehot_ready = sem("onehot_ready")
        pair_free = sem("pair_free")
        agg_ready = sem("agg_ready")
        agg_free = sem("agg_free")

        def before(n):
            return NAMES.index(n)

        S = {}
        for n in NAMES:
            for what in ("table_ready", "table_stored", "dve_steps"):
                S[n, what] = sem(f"{n}_{what}")
        norm = ("var_ready", "std_ready")
        product = ("rows_ready", "rows_turned", "turned_copied", "product_ready", "dve_steps2")
        second = ("normed_ready", "normed_turned", "normed_copied")
        ys = ("y_ready", "y_added", "y_in_sbuf")
        for n, names in {"sage": product + norm + second + ("self_copied", "square_ready", "length_ready",
                                                            "degree_ready", "degree_root", "product2_ready",
                                                            "product2_free", "dve_steps3"),
                         "gcn2": product + norm, "hop2": product + norm + second + ys,
                         "rel1": product + ys}.items():
            for what in names:
                S[n, what] = sem(f"{n}_{what}")

        block = ctx.enter_context(nc.Block())

        def xt(t):
            return x_sb[:, bass.ds(t * D, D)]

        def ht(t):
            return h_sb[:, bass.ds(t * D, D)]

        def tt(t, w=D):
            return t_sb[:, bass.ds(t * D, w)]

        def over_tiles(eng, visits, parts):
            start = max([lag for lag, _ in parts], default=0)
            start += (TILES - start) % 2

            def round_(tile, bank, known):
                if known is None or known < TILES:
                    visits(tile(0), bank)
                for lag, part in parts:
                    if known is None or 0 <= known - lag < TILES:
                        part(tile(lag), (bank - lag) % 2)

            for i in range(start):
                round_(lambda lag, i=i: i - lag, i % 2, i)
            with eng.Fori(0, (TILES - start) // 2) as j:
                for k in range(2):
                    round_(lambda lag, k=k: j * 2 + (start + k - lag), (start + k) % 2, None)
            for i in range(TILES, TILES + max([lag for lag, _ in parts], default=0)):
                round_(lambda lag, i=i: i - lag, i % 2, i)

        def out_of_order(eng):
            return eng.value_load(flag[0:1, 0:1], min_val=0, max_val=CHUNKS * P)

        @block.sync
        def _(sp):
            for lo in range(0, TILES - 1, 8):
                hi = min(lo + 8, TILES - 1)
                sp.dma_start(x_sb[:, lo * D:hi * D].rearrange("p (t d) -> p t d", d=D),
                             x[lo * P:hi * P].rearrange("(t p) d -> p t d", p=P)).then_inc(s_x, 16)
            sp.wait_ge(s_pad, 1)
            sp.dma_start(x_sb[0:LAST, (TILES - 1) * D:TILES * D], x[(TILES - 1) * P:N]).then_inc(s_x, 16)
            for k, w in enumerate((w_self, w_neigh, hop_w)):
                sp.dma_start(wraw[:, k * KB * D:(k + 1) * KB * D].rearrange("p (m i) -> p m i", m=KB),
                             w.rearrange("(m p) i -> p m i", p=P)).then_inc(s_w, 16)
            sp.dma_start(w1_sb[:], gcn_w1.rearrange("(k p) o -> p k o", p=P)).then_inc(s_w, 16)
            sp.dma_start(w2_sb[:], gcn_w2).then_inc(s_w, 16)
            sp.dma_start(b1_sb[:], gcn_b1.partition_broadcast(P)).then_inc(s_w, 16)
            sp.dma_start(b2_sb[:], gcn_b2.partition_broadcast(P)).then_inc(s_w, 16)
            sp.dma_start(hopb_sb[:], hop_b.partition_broadcast(P)).then_inc(s_w, 16)

            def load_relations(w, b, s):
                for j in range(2):
                    sp.dma_start(relb_sb[:, j, :], b.partition_broadcast(P)).then_inc(s, 16)
                for k in range(KB):
                    sp.dma_start(relw[:, k, :, :], w[:, k * P:(k + 1) * P, :].rearrange("r p o -> p r o")
                                 ).then_inc(s, 16)

            load_relations(rel_w0, rel_b0, s_wrel[0])

            sp.wait_ge(s_flag, 1)
            with sp.If(out_of_order(sp) > 0):
                sp.wait_ge(s_scat, 16 * CHUNKS)
                for b in range(QB):
                    sp.dma_start(flat_s[:, b * 4 * P:(b + 1) * 4 * P],
                                 sorted_dram[b * QP * P:(b + 1) * QP * P].rearrange("(q e) f -> q (e f)", q=QP)
                                 ).then_inc(s_srt, 16)

            for pi, n in enumerate(NAMES):
                if n == "rel1":
                    sp.wait_ge(S["rel1", "table_stored"], 16 * TILES + 1)
                    load_relations(rel_w1, rel_b1, s_wrel[1])
                if pi == 0:
                    sp.sem_inc(quad_landed, AHEAD)
                with sp.Fori(0, ROUNDS) as r:
                    for k in range(GQ):
                        sp.wait_ge(s_land[k], (r + (1 + pi * ROUNDS)) * (16 * QUAD))
                        sp.sem_inc(quad_landed, 1)
            sp.wait_ge(s_out, 16 * TILES)

        @block.gpsimd
        def _(pool):
            nc.gpsimd.memset(flat_i[:, 0:QB * P], 0).then_inc(s_fill, 1)
            nc.gpsimd.memset(flat_i[:, QB * P:2 * QB * P], int(PAD_DST)).then_inc(s_fill, 1)
            nc.gpsimd.memset(flat_i[:, 2 * QB * P:3 * QB * P], 0).then_inc(s_fill, 1)
            nc.gpsimd.memset(flat_w, 0.0).then_inc(s_fill, 1)
            nc.gpsimd.memset(flat_next, int(PAD_DST)).then_inc(s_fill, 1)
            nc.gpsimd.memset(x_sb[:, (TILES - 1) * D:TILES * D], 0.0).then_inc(s_fill, 1)
            pool.wait_ge(s_fill, 6)
            pool.sem_inc(s_pad, 1)
            nc.gpsimd.iota(iota[:], pattern=[[1, NPAD]], base=0, channel_multiplier=0,
                           allow_small_or_imprecise_dtypes=True).then_inc(s_const, 1)
            nc.gpsimd.memset(ident[:], 0.0).then_inc(s_fill, 1)
            nc.gpsimd.memset(lower[:], 0.0).then_inc(s_fill, 1)
            pool.wait_ge(s_fill, 8)
            nc.gpsimd.affine_select(out=ident[:], in_=ident[:], compare_op=ALU.not_equal, fill=1.0,
                                    base=0, pattern=[[-1, P]], channel_multiplier=1).then_inc(s_const, 1)
            nc.gpsimd.affine_select(out=lower[:], in_=lower[:], compare_op=ALU.is_ge, fill=1.0,
                                    base=0, pattern=[[-1, P]], channel_multiplier=1).then_inc(s_const, 1)
            nc.gpsimd.memset(ones[:], 1.0).then_inc(s_const, 1)
            nc.gpsimd.memset(eps[:], LN_EPS).then_inc(s_const, 1)

            pool.wait_ge(s_flag, 1)
            with pool.If(out_of_order(pool) > 0):
                pool.wait_ge(s_pos, 1)
                with pool.Fori(0, BLOCKS) as r:
                    nc.gpsimd.tensor_copy(stage_idx[:, 0, :], pos_u[:, bass.ds(r * STAGE, STAGE)]
                                          ).then_inc(s_scat_stage, 1)
                    nc.gpsimd.tensor_copy(stage_rec[:].rearrange("p (c f) -> p c f", f=4),
                                          edges[:, bass.ds(r * STAGE, STAGE), :]).then_inc(s_scat_stage, 1)
                    pool.wait_ge(s_scat_stage, r * 2 + 2)
                    pool.sem_inc(s_passed[0], 1)
                    for k in range(STAGE):
                        pool.indirect_dma_start(
                            sorted_dram, bass.IndirectOffsetOnAxis(ap=stage_idx[:, 0, k:k + 1], axis=0),
                            stage_rec[:, k * 4:(k + 1) * 4], None).then_inc(s_scat, 16)
                    pool.wait_ge(s_scat, r * (16 * STAGE) + 16 * STAGE)

            pool.wait_ge(s_idx, 2)
            for pi, n in enumerate(NAMES):
                width = PASSES[n][1]
                index = idx_rel if n in ("rel1", "rel2") else idx_node
                pool.wait_ge(S[n, "table_stored"], 16 * (TILES // GROUP) if n == "sage" else 16 * TILES + 1)
                with pool.Fori(0, ROUNDS) as r:
                    for h in range(2):
                        pool.wait_ge(quad_landed, r * GQ + (pi * QUADS + h * QUAD + 1))
                        nc.gpsimd.tensor_copy(stage_idx[:, h, :],
                                              index[:, bass.ds(r * GRING + h * STAGE, STAGE)]).then_inc(s_stage, 1)
                        pool.wait_ge(s_stage, r * 2 + (2 * ROUNDS * pi + h + 1))
                        for k in range(STAGE):
                            slot = h * STAGE + k
                            if k % QUAD == 0:
                                pool.wait_ge(quad_free, r * GQ + (pi * (QUADS - 1) + slot // QUAD + 1))
                                pool.sem_inc(s_passed[0], 1)
                            pool.indirect_dma_start(
                                gathered[:, slot * D:slot * D + width], None, tables[n],
                                bass.IndirectOffsetOnAxis(ap=stage_idx[:, h, k:k + 1], axis=0)
                            ).then_inc(s_land[slot // QUAD], 16)

        def bounds_of(eng, t):
            first = eng.value_load(bounds[0:1, bass.ds(t, 1)], min_val=0, max_val=QUADS - 1)
            last = eng.value_load(bounds[0:1, bass.ds(t + 1, 1)], min_val=0, max_val=QUADS - 1)
            return first, last

        @block.tensor
        def _(pe):
            pe.wait_ge(s_const, 5)
            def turn_edges(rows, first):
                for b in range(QB):
                    if first + b >= 2:
                        pe.wait_ge(s_edgef, first + b - 1)
                    for f in range(4):
                        mm = pe.transpose(y_ps[b % 2][0:P, f // 2, (f % 2) * P:(f % 2) * P + QP],
                                          rows(b, f), ident[0:QP, 0:QP])
                    mm.then_inc(s_flat_t, 1)

            pe.wait_ge(s_drops, 1)
            pe.matmul(prod2[:, 0:1], ones[0:QP, :], drops[0:QP, 0:1], start=True, stop=True).then_inc(s_dropmm, 1)
            pe.wait_ge(s_flat, 1)
            turn_edges(lambda b, f: flat_f[:, (f * QB + b) * P:(f * QB + b + 1) * P], 0)

            pe.wait_ge(s_flag, 1)
            with pe.If(out_of_order(pe) > 0):
                pe.wait_ge(s_tot, 1)
                pe.matmul(prod[:, 0:BUCKETS], ones[:], tot, start=True, stop=True)
                pe.matmul(prod[:, 64:64 + BUCKETS], lower[:], tot, start=True, stop=True).then_inc(s_totmm, 1)
                pe.wait_ge(s_srt, 16 * QB)
                turn_edges(lambda b, f: flat_s[:, b * 4 * P:(b + 1) * 4 * P].rearrange("q (e f) -> q f e", f=4)[:, f, :],
                           QB)

            pe.wait_ge(s_tot2, 1)
            pe.matmul(prod2[:, 0:BUCKETS], ones[:], tot, start=True, stop=True).then_inc(s_totmm2, 1)

            pe.wait_ge(s_w, 16 * 8)
            for k in range(3):
                if k >= 1:
                    pe.wait_ge(s_wtc, k)
                for m in range(KB):
                    for j in range(KB):
                        mm = pe.transpose(turn_ps[:, j * KB + m, :],
                                          wraw[:, (k * KB + m) * D + j * P:(k * KB + m) * D + (j + 1) * P], ident[:])
                mm.then_inc(s_wt, 1)
            pe.wait_ge(s_wtc, 3)
            pe.wait_ge(s_bounds, 1)

            def visits_of(n):
                weighted, width = PASSES[n]
                per = 2 if n == "sage" else 1

                quads0, visits0, tiles0 = before(n) * QUADS, before(n) * VISITS, before(n) * TILES
                made0 = before(n) and (before(n) + 1) * VISITS * QUAD

                def group(q, t, b, first):
                    u = q + t
                    pe.wait_ge(quad_landed, q + (quads0 + AHEAD + 1))
                    for k in range(QUAD):
                        pe.wait_ge(onehot_ready, u * (QUAD * per) + (made0 + (k + 1) * per))
                        mm = pe.matmul(agg[b][:, 0:width], onehot[:, k * P:(k + 1) * P],
                                       gathered[:, bass.ds((q & (GQ - 1)) * (QUAD * D) + k * D, width)],
                                       start=first and k == 0, stop=True, skip_group_check=True)
                        if n == "sage":
                            mm = pe.matmul(agg[b][:, D:D + 4], onehot1[:, k * P:(k + 1) * P],
                                           one_w[:, bass.ds(q * QUAD + k, 1), :].rearrange("p c k -> p (c k)"),
                                           start=False, stop=True, skip_group_check=True)
                        if k % 2 == 1:
                            mm.then_inc(pair_free, 1)
                        elif k == 0 and not first:
                            mm.then_inc(quad_free, 1)

                def visits(t, b):
                    lo, hi = bounds_of(pe, t)
                    pe.wait_ge(agg_free, t + (tiles0 + 1))
                    group(lo, t, b, True)
                    with pe.If(lo < hi):
                        with pe.Fori(lo + 1, hi + 1) as q:
                            group(q, t, b, False)
                    pe.drain().then_inc(agg_ready, 1)
                return visits

            def turn(n, rows, t):
                pe.wait_ge(S[n, "rows_ready"], t + 1)
                for k, r in enumerate(rows):
                    mm = pe.transpose(turn_ps[:, k, :], r, ident[:])
                mm.then_inc(S[n, "rows_turned"], 1)
                pe.wait_ge(S[n, "turned_copied"], t + 1)

            def turn_normed(n, t):
                pe.wait_ge(S[n, "normed_ready"], t + 1)
                for k in range(KB):
                    mm = pe.transpose(turn_ps[:, k, :], normed[:, k * P:(k + 1) * P], ident[:])
                mm.then_inc(S[n, "normed_turned"], 1)
                pe.wait_ge(S[n, "normed_copied"], t + 1)

            def product(to, rows_t, blocks, done):
                for k, w in enumerate(blocks):
                    mm = pe.matmul(to, rows_t[:, k, :], w, start=(k == 0), stop=(k == len(blocks) - 1))
                mm.then_inc(done, 1)

            def relations(n, rows_t, t):
                for g in range(REL // 2):
                    pe.wait_ge(S[n, "y_added"], t * (REL // 2) + (g + 1))
                    for k in range(KB):
                        mm = pe.matmul(y_ps[g % 2][:], rows_t[:, k, :], relw[:, k, 2 * g:2 * g + 2, :],
                                       start=(k == 0), stop=(k == KB - 1))
                    mm.then_inc(S[n, "y_ready"], 1)

            halves = [post[:, k * P:(k + 1) * P] for k in range(KB)]
            selfs = [post2[:, k * P:(k + 1) * P] for k in range(KB)]

            def sage_rows(t, b):
                pe.wait_ge(S["sage", "self_copied"], t + 1)
                turn("sage", halves + selfs, t)
                product(prod[:, 0:D], turned, [wneigh_t[:, k, :] for k in range(KB)]
                        + [wself_t[:, k, :] for k in range(KB)], S["sage", "product_ready"])

            def sage_normed(t, b):
                turn_normed("sage", t)
                pe.wait_ge(S["sage", "product2_free"], t + 1)
                product(prod2[:, 0:HID], normed_t, [w1_sb[:, k, :] for k in range(KB)], S["sage", "product2_ready"])

            def gcn2_rows(t, b):
                turn("gcn2", halves[0:1], t)
                product(prod[:, 0:D], turned, [w2_sb[:]], S["gcn2", "product_ready"])

            def hop2_rows(t, b):
                turn("hop2", halves, t)
                product(prod[:, 0:D], turned, [hopw_t[:, k, :] for k in range(KB)], S["hop2", "product_ready"])

            def hop2_normed(t, b):
                turn_normed("hop2", t)
                relations("hop2", normed_t, t)

            def rel1_rows(t, b):
                turn("rel1", halves, t)
                relations("rel1", turned, t)

            parts = {"sage": [(3, sage_normed), (1, sage_rows)], "gcn1": [], "gcn2": [(1, gcn2_rows)],
                     "hop1": [], "hop2": [(3, hop2_normed), (1, hop2_rows)], "rel1": [(1, rel1_rows)],
                     "rel2": []}
            pe.sem_inc(pair_free, 2)
            pe.sem_inc(quad_free, GQ)
            pe.sem_inc(agg_free, 2)
            for n in NAMES:
                if n in ("hop2", "rel1"):
                    pe.sem_inc(S[n, "y_added"], 2)
                    pe.wait_ge(s_wrel[0 if n == "hop2" else 1], 16 * (KB + 2))
                if n == "sage":
                    pe.sem_inc(S[n, "product2_free"], 1)
                if n in ("sage", "gcn2", "hop2", "rel1"):
                    pe.sem_inc(S[n, "rows_turned"], 1)
                if n in ("sage", "hop2"):
                    pe.sem_inc(S[n, "normed_turned"], 1)
                over_tiles(pe, visits_of(n), parts[n])

        @block.scalar
        def _(act):
            act.wait_ge(s_pad, 1)
            full = (CHUNKS - QP) * P
            for a, to, off in ((dst, flat_i[:, F:2 * F], 0), (dst, flat_next, 1), (src, flat_i[:, 0:F], 0),
                               (edge_type, flat_i[:, 2 * F:3 * F], 0), (edge_weight, flat_w, 0)):
                act.dma_start(to[:, 0:F - P].rearrange("q (b e) -> q b e", e=P),
                              a[off:off + full].rearrange("(b q e) -> q b e", q=QP, e=P)).then_inc(s_edge, 16)
                act.dma_start(to[0:QP - 1, F - P:F],
                              a[off + full:off + full + (QP - 1) * P].rearrange("(q e) -> q e", e=P)
                              ).then_inc(s_edge, 16)
                act.dma_start(to[QP - 1:QP, F - P:F - P + TAIL - off],
                              a[off + full + (QP - 1) * P:E].rearrange("(q e) -> q e", q=1)).then_inc(s_edge, 16)

            act.wait_ge(s_const, 5)
            act.wait_ge(s_mv, TILES)
            nc.scalar.activation(rstd_all[:], mv_all[:, :, 1], ACT.Sqrt, bias=eps[:]).then_inc(s_std, 1)
            act.wait_ge(s_rstd, 1)
            with act.Fori(0, TILES // GROUP) as g:
                for k in range(GROUP):
                    t = g * GROUP + k
                    act.wait_ge(s_shift, t + 1)
                    nc.scalar.activation(ht(t), ht(t), ACT.Copy, scale=rstd_all[:, bass.ds(t, 1)]).then_inc(s_scaled, 1)
                act.wait_ge(s_scaled, g * GROUP + GROUP)
                act.dma_start(tables["sage"].rearrange("(t p) d -> p t d", p=P)[:, bass.ds(g * GROUP, GROUP), :],
                              h_sb[:, bass.ds(g * (GROUP * D), GROUP * D)].rearrange("p (t d) -> p t d", d=D)
                              ).then_inc(S["sage", "table_stored"], 16)
            for k, w in enumerate((wself_t, wneigh_t, hopw_t)):
                act.wait_ge(s_wt, k + 1)
                nc.scalar.copy(w[:].rearrange("p k o -> p (k o)"),
                               turn_ps[:].rearrange("p k o -> p (k o)")).then_inc(s_wtc, 1)
            for n in NAMES[1:]:
                act.sem_inc(S[n, "table_stored"], 1)

            def copy_turned(n, blocks, t):
                act.wait_ge(S[n, "rows_turned"], t + 2)
                nc.scalar.copy(turned[:, 0:blocks, :].rearrange("p k o -> p (k o)"),
                               turn_ps[:, 0:blocks, :].rearrange("p k o -> p (k o)")
                               ).then_inc(S[n, "turned_copied"], 1)

            def copy_normed(n, t):
                act.wait_ge(S[n, "normed_turned"], t + 2)
                nc.scalar.copy(normed_t[:].rearrange("p k o -> p (k o)"),
                               turn_ps[:, 0:KB, :].rearrange("p k o -> p (k o)")).then_inc(S[n, "normed_copied"], 1)

            def root(n, t):
                act.wait_ge(S[n, "var_ready"], t + 1)
                nc.scalar.activation(small[:, 2:3], small[:, 1:2], ACT.Sqrt, bias=eps[:]
                                     ).then_inc(S[n, "std_ready"], 1)

            def store(n, to, t):
                act.wait_ge(S[n, "table_ready"], t + 1)
                act.dma_start(tables[to][bass.ds(t * P, P), :], tt(t, PASSES[to][1])
                              ).then_inc(S[to, "table_stored"], 16)

            def finish_relations(n, to, t):
                act.wait_ge(S[n, "y_added"], t * (REL // 2) + (REL // 2 + 2))
                nc.scalar.activation(y_sb[:].rearrange("p r d -> p (r d)"), y_sb[:].rearrange("p r d -> p (r d)"),
                                     ACT.Relu).then_inc(S[n, "y_in_sbuf"], 1)
                act.wait_ge(S[n, "y_in_sbuf"], t + 1)
                act.dma_start(tables[to].rearrange("(r n) d -> n r d", r=REL)[bass.ds(t * P, P), :, :], y_sb[:]
                              ).then_inc(S[to, "table_stored"], 16)

            def sage_rows(t, b):
                n = "sage"
                nc.scalar.copy(post2[:], ht(t)).then_inc(S[n, "self_copied"], 1)
                act.wait_ge(S[n, "degree_ready"], t + 1)
                nc.scalar.activation(small[:, 10:12], small[:, 8:10], ACT.Sqrt).then_inc(S[n, "degree_root"], 1)
                copy_turned(n, 4, t)
                act.wait_ge(S[n, "product_ready"], t + 1)
                nc.scalar.activation(y_sb[:, 0, :], prod[:, 0:D], ACT.Square, accum_out=small[:, 4:5]
                                     ).then_inc(S[n, "square_ready"], 1)
                act.wait_ge(S[n, "square_ready"], t + 1)
                nc.scalar.activation(small[:, 5:6], small[:, 4:5], ACT.Sqrt).then_inc(S[n, "length_ready"], 1)

            parts = {
                "sage": [(3, lambda t, b: copy_normed("sage", t)), (2, lambda t, b: root("sage", t)), (1, sage_rows),
                         (3, lambda t, b: store("sage", "gcn1", t))],
                "gcn1": [(1, lambda t, b: store("gcn1", "gcn2", t))],
                "gcn2": [(2, lambda t, b: root("gcn2", t)), (1, lambda t, b: copy_turned("gcn2", 1, t)),
                         (2, lambda t, b: store("gcn2", "hop1", t))],
                "hop1": [(1, lambda t, b: store("hop1", "hop2", t))],
                "hop2": [(3, lambda t, b: copy_normed("hop2", t)), (2, lambda t, b: root("hop2", t)),
                         (1, lambda t, b: copy_turned("hop2", 2, t)),
                         (3, lambda t, b: finish_relations("hop2", "rel1", t))],
                "rel1": [(1, lambda t, b: copy_turned("rel1", 2, t)),
                         (1, lambda t, b: finish_relations("rel1", "rel2", t))],
            }
            for n in NAMES[:-1]:
                over_tiles(act, lambda t, b: None, parts[n])
            with act.Fori(0, TILES - 1) as t:
                act.wait_ge(S["rel2", "table_ready"], t + 1)
                act.dma_start(out[bass.ds(t * P, P), :], xt(t)).then_inc(s_out, 16)
            act.wait_ge(S["rel2", "table_ready"], TILES)
            act.dma_start(out[(TILES - 1) * P:N, :], x_sb[0:LAST, (TILES - 1) * D:TILES * D]).then_inc(s_out, 16)

        @block.vector
        def _(dve):
            prep = Steps(dve, s_prep, 0, 0)

            dve.wait_ge(s_edge, 16 * 15)
            prep(nc.vector.tensor_tensor(drop, flat_i[:, F:2 * F], flat_next, ALU.is_gt))
            nc.vector.tensor_reduce(drops[0:QP, 0:1], drop, AXX, ALU.add).then_inc(s_drops, 1)
            for f, k in ((0, 0), (1, 1), (3, 2)):
                prep(nc.vector.tensor_copy(flat_f[:, f * F:(f + 1) * F], flat_i[:, k * F:(k + 1) * F]))
            nc.vector.tensor_copy(flat_f[:, 2 * F:3 * F], flat_w).then_inc(s_flat, 1)
            dve.wait_ge(s_dropmm, 1)
            nc.vector.tensor_copy(flag[:], prod2[:, 0:1]).then_inc(s_flag, 1)

            dve.wait_ge(s_x, 16 * X_LOADS)
            with dve.Fori(0, TILES // GROUP) as g:
                for k in range(GROUP):
                    t = g * GROUP + k
                    nc.vector.bn_stats(bn_all[:, bass.ds(t, 1), :].rearrange("p a s -> p (a s)"), xt(t)
                                       ).then_inc(s_bn, 1)
            dve.wait_ge(s_bn, TILES)
            for t in range(TILES):
                nc.vector.bn_aggr(mv_all[:, t, :], bn_all[:, t, :]).then_inc(s_mv, 1)

            def copy_edges(first):
                for b in range(QB):
                    dve.wait_ge(s_flat_t, first + b + 1)
                    nc.vector.tensor_copy(
                        edges[:, b * QP:(b + 1) * QP, :],
                        y_ps[b % 2][:].rearrange("p a (g e) -> p e (a g)", g=2)[:, 0:QP, :]
                    ).then_inc(s_edgef, 1)
                dve.wait_ge(s_edgef, first + QB)

            copy_edges(0)

            dve.wait_ge(s_std, 1)
            nc.vector.reciprocal(rstd_all[:], rstd_all[:]).then_inc(s_rstd, 1)
            with dve.Fori(0, TILES // GROUP) as g:
                for k in range(GROUP):
                    t = g * GROUP + k
                    nc.vector.tensor_scalar(ht(t), xt(t), mv_all[:, bass.ds(t, 1), 0:1].rearrange("p a s -> p (a s)"),
                                            0.0, ALU.subtract, ALU.max).then_inc(s_shift, 1)

            dve.wait_ge(s_const, 5)

            def bucket_totals(s_prep_, s_steps):
                prep = Steps(dve, s_prep_, 0, 0)
                prep(nc.vector.tensor_copy(tile_i, edges[:, :, 1]))
                prep(nc.vector.tensor_scalar(tile_i, tile_i, TSHIFT, None, ALU.logical_shift_right))
                prep(nc.vector.tensor_copy(tile_f, tile_i))
                prep(nc.vector.tensor_scalar(tile_f, tile_f, float(TILES), None, ALU.min))
                with dve.Fori(0, BUCKETS) as t:
                    step = Steps(dve, s_steps, 2, t)
                    step(nc.vector.tensor_scalar(mask, tile_f, iota[:, bass.ds(t, 1)], None, ALU.is_equal))
                    step(nc.vector.tensor_reduce(tot[:, bass.ds(t, 1)], mask, AXX, ALU.add))
                    step.close()

            def bucket_ends(prep, sums):
                prep(nc.vector.memset(ends[0][:, 0:32], 0.0))
                prep(nc.vector.memset(ends[1][:, 0:32], 0.0))
                prep(nc.vector.tensor_copy(ends[0][:, 32:], sums))
                for j in range(5):
                    a, b = ends[j % 2], ends[(j + 1) % 2]
                    prep(nc.vector.tensor_tensor(b[:, 32:], a[:, 32:], a[:, 32 - (1 << j):-(1 << j)], ALU.add))
                return ends[1][:, 32:]

            dve.wait_ge(s_flag, 1)
            with dve.If(out_of_order(dve) > 0):
                bucket_totals(s_sort_prep, s_total_steps)
                dve.sem_inc(s_tot, 1)
                dve.wait_ge(s_totmm, 1)
                sort = Steps(dve, s_sort, 0, 0)
                end = bucket_ends(sort, prod[:, 0:BUCKETS])
                sort(nc.vector.tensor_copy(totals, prod[:, 0:BUCKETS]))
                sort(nc.vector.tensor_tensor(base, end, totals, ALU.subtract))
                sort(nc.vector.scalar_tensor_tensor(base, base, -1.0, prod[:, 64:64 + BUCKETS], ALU.add, ALU.add))
                sort(nc.vector.memset(scan[0][:, 0:256], 0.0))
                sort(nc.vector.memset(scan[1][:, 0:256], 0.0))
                sort(nc.vector.memset(pos, 0.0))
                with dve.Fori(0, BUCKETS) as t:
                    step = Steps(dve, s_rank, 13, t)
                    step(nc.vector.tensor_scalar(scan[0][:, 256:], tile_f, iota[:, bass.ds(t, 1)], None, ALU.is_equal))
                    step(nc.vector.tensor_copy(mask, scan[0][:, 256:]))
                    for j in range(9):
                        a, b = scan[j % 2], scan[(j + 1) % 2]
                        step(nc.vector.tensor_tensor(b[:, 256:], a[:, 256:], a[:, 256 - (1 << j):-(1 << j)], ALU.add))
                    step(nc.vector.scalar_tensor_tensor(mask, scan[1][:, 256:], base[:, bass.ds(t, 1)], mask,
                                                        ALU.add, ALU.mult))
                    step(nc.vector.tensor_tensor(pos, pos, mask, ALU.add))
                    step.close()
                sort(nc.vector.tensor_copy(pos_u, pos))
                dve.sem_inc(s_pos, 1)
                copy_edges(QB)

            nc.vector.tensor_copy(idx_node[:], edges[:, :, 0]).then_inc(s_idx, 1)
            nc.vector.scalar_tensor_tensor(idx_rel[:], edges[:, :, 3], float(NPAD), edges[:, :, 0],
                                           ALU.mult, ALU.add).then_inc(s_idx, 1)
            nc.vector.memset(one_w[:, :, 0], 1.0).then_inc(s_idx, 1)
            prep(nc.vector.tensor_copy(one_w[:, :, 1], edges[:, :, 2]))
            prep(nc.vector.tensor_tensor(rest_w, edges[:, :, 2], one_w[:, :, 1], ALU.subtract))
            prep(nc.vector.tensor_copy(one_w[:, :, 2], rest_w))
            prep(nc.vector.tensor_tensor(rest_w2, rest_w, one_w[:, :, 2], ALU.subtract))
            prep(nc.vector.tensor_copy(one_w[:, :, 3], rest_w2))

            bucket_totals(s_order_prep, s_total_steps2)
            dve.sem_inc(s_tot2, 1)
            dve.wait_ge(s_totmm2, 1)
            end = bucket_ends(prep, prod2[:, 0:BUCKETS])
            prep(nc.vector.tensor_copy(ends_i, end))
            prep(nc.vector.tensor_scalar(ends_i, ends_i, SHIFT, None, ALU.logical_shift_right))
            prep(nc.vector.memset(bounds[:], 0))
            prep(nc.vector.tensor_copy(bounds[:, 1:], ends_i[:, 0:TILES]))
            dve.sem_inc(s_bounds, 1)
            dve.wait_ge(s_wtc, 3)

            def norm(n, step, rows, to):
                dve.sem_inc(s_passed[1], 1)
                step(nc.vector.bn_stats(bnst[:], rows))
                dve.sem_inc(s_passed[1], 1)
                nc.vector.bn_aggr(small[:, 0:2], bnst[:]).then_inc(S[n, "var_ready"], 1)
                dve.wait_ge(S[n, "std_ready"], step.t + 1)
                step(nc.vector.reciprocal(small[:, 3:4], small[:, 2:3]))
                step(nc.vector.tensor_scalar(post2n[:], rows, small[:, 0:1], 0.0, ALU.subtract, ALU.max))
                step(nc.vector.tensor_scalar(to, post2n[:], small[:, 3:4], None, ALU.mult))

            def visits_of(n):
                weighted = PASSES[n][0]

                def visits(t, b):
                    lo, hi = bounds_of(dve, t)
                    with dve.Fori(lo, hi + 1) as q:
                        u = q + t
                        for k in range(QUAD):
                            if k % 2 == 0:
                                dve.wait_ge(pair_free, u * 2 + (before(n) * 2 * VISITS + k // 2 + 1))
                            edge = edges[:, bass.ds(q * QUAD + k, 1), :].rearrange("p c f -> p (c f)")
                            places = iota[:, bass.ds(t * P, P)]
                            to = onehot[:, k * P:(k + 1) * P]
                            if n == "sage":
                                nc.vector.tensor_scalar(onehot1[:, k * P:(k + 1) * P], places, edge[:, 1:2], None,
                                                        ALU.is_equal).then_inc(onehot_ready, 1)
                            if weighted:
                                ins = nc.vector.tensor_scalar(to, places, edge[:, 1:2], edge[:, 2:3],
                                                              ALU.is_equal, ALU.mult)
                            else:
                                ins = nc.vector.tensor_scalar(to, places, edge[:, 1:2], None, ALU.is_equal)
                            ins.then_inc(onehot_ready, 1)
                return visits

            def d(t, k):
                return dinv[:, bass.ds(t, 1), k:k + 1].rearrange("p a b -> p (a b)")

            def half_d(t):
                return hdinv[:, bass.ds(t, 1)]

            def rows_free(n, t):
                dve.wait_ge(S[n, "rows_turned"], t + 1)

            def normed_free(n, t):
                dve.wait_ge(S[n, "normed_turned"], t + 1)

            def relations(n, t):
                dve.wait_ge(S[{"hop2": "rel1", "rel1": "rel2"}[n], "table_stored"], t * 16 + 1)
                for g in range(REL // 2):
                    dve.wait_ge(S[n, "y_ready"], t * (REL // 2) + (g + 1))
                    nc.vector.tensor_tensor(y_sb[:, 2 * g:2 * g + 2, :], y_ps[g % 2][:], relb_sb[:], ALU.add
                                            ).then_inc(S[n, "y_added"], 1)

            def sage_rows(t, b):
                n = "sage"
                step = Steps(dve, S[n, "dve_steps"], 5, t)
                dve.wait_ge(agg_ready, t + (before(n) * TILES + 1))
                rows_free(n, t)
                step(nc.vector.tensor_copy(post[:], agg[b][:, 0:D]))
                dve.sem_inc(S[n, "rows_ready"], 1)
                step(nc.vector.tensor_copy(small[:, 12:13], agg[b][:, D:D + 1]))
                step(nc.vector.tensor_reduce(small[:, 13:14], agg[b][:, D + 1:D + 4], AXX, ALU.add))
                dve.sem_inc(agg_free, 1)
                step(nc.vector.tensor_scalar(small[:, 6:8], small[:, 12:14], 1.0, None, ALU.add))
                step(nc.vector.tensor_scalar(small[:, 8:10], small[:, 6:8], DEG_EPS, None, ALU.max))
                dve.sem_inc(S[n, "degree_ready"], 1)

            def sage_product(t, b):
                n = "sage"
                step = Steps(dve, S[n, "dve_steps2"], 10, t)
                dve.wait_ge(S[n, "degree_root"], t + 1)
                step(nc.vector.reciprocal(small[:, 12:14], small[:, 10:12]))
                dt_ = dinv[:, bass.ds(t, 1), :].rearrange("p a b -> p (a b)")
                step(nc.vector.scalar_tensor_tensor(dt_, small[:, 6:8], 0.0, small[:, 12:14], ALU.is_gt, ALU.mult))
                step(nc.vector.tensor_scalar(half_d(t), d(t, 1), 0.5, None, ALU.mult))
                dve.wait_ge(S[n, "length_ready"], t + 1)
                step(nc.vector.tensor_scalar(small[:, 14:15], small[:, 5:6], NORM_EPS, None, ALU.max))
                step(nc.vector.reciprocal(small[:, 15:16], small[:, 14:15]))
                step(nc.vector.scalar_tensor_tensor(xt(t), prod[:, 0:D], small[:, 15:16], xt(t), ALU.mult, ALU.add))
                normed_free(n, t)
                norm(n, step, xt(t), normed[:])
                dve.sem_inc(S[n, "normed_ready"], 1)
                step.close()

            def sage_table(t, b):
                n = "sage"
                step = Steps(dve, S[n, "dve_steps3"], 1, t)
                dve.wait_ge(S[n, "product2_ready"], t + 1)
                step(nc.vector.tensor_scalar(tt(t, HID), prod2[:, 0:HID], d(t, 0), None, ALU.mult))
                dve.sem_inc(S[n, "table_ready"], 1)
                dve.sem_inc(S[n, "product2_free"], 1)
                step.close()

            def gcn1_rows(t, b):
                n = "gcn1"
                step = Steps(dve, S[n, "dve_steps"], 4, t)
                dve.wait_ge(agg_ready, t + (before(n) * TILES + 1))
                step(nc.vector.tensor_tensor(post[:, 0:HID], agg[b][:, 0:HID], tt(t, HID), ALU.add))
                dve.sem_inc(agg_free, 1)
                step(nc.vector.tensor_scalar(post[:, 0:HID], post[:, 0:HID], d(t, 0), None, ALU.mult))
                step(nc.vector.tensor_tensor(post[:, 0:HID], post[:, 0:HID], b1_sb[:], ALU.add))
                step(nc.vector.tensor_scalar(tt(t, HID), post[:, 0:HID], 0.0, d(t, 0), ALU.max, ALU.mult))
                dve.sem_inc(S[n, "table_ready"], 1)
                step.close()

            def gcn2_rows(t, b):
                n = "gcn2"
                step = Steps(dve, S[n, "dve_steps"], 2, t)
                dve.wait_ge(agg_ready, t + (before(n) * TILES + 1))
                rows_free(n, t)
                step(nc.vector.tensor_tensor(post[:, 0:HID], agg[b][:, 0:HID], tt(t, HID), ALU.add))
                dve.sem_inc(agg_free, 1)
                step(nc.vector.tensor_scalar(post[:, 0:HID], post[:, 0:HID], d(t, 0), None, ALU.mult))
                dve.sem_inc(S[n, "rows_ready"], 1)
                step.close()

            def gcn2_product(t, b):
                n = "gcn2"
                step = Steps(dve, S[n, "dve_steps2"], 7, t)
                step(nc.vector.tensor_tensor(xt(t), xt(t), b2_sb[:], ALU.add))
                dve.wait_ge(S[n, "product_ready"], t + 1)
                step(nc.vector.tensor_tensor(xt(t), prod[:, 0:D], xt(t), ALU.add))
                norm(n, step, xt(t), ht(t))
                step(nc.vector.tensor_scalar(tt(t), ht(t), d(t, 1), None, ALU.mult))
                dve.sem_inc(S[n, "table_ready"], 1)
                step.close()

            def hop(step, n, t, b):
                dve.wait_ge(agg_ready, t + (before(n) * TILES + 1))
                if n == "hop2":
                    rows_free(n, t)
                step(nc.vector.tensor_tensor(post[:], agg[b][:, 0:D], tt(t), ALU.add))
                dve.sem_inc(agg_free, 1)
                if n == "hop1":
                    step(nc.vector.tensor_scalar(ht(t), ht(t), 0.5, None, ALU.mult))
                step(nc.vector.scalar_tensor_tensor(post[:], post[:], half_d(t), ht(t), ALU.mult, ALU.add))

            def hop1_rows(t, b):
                step = Steps(dve, S["hop1", "dve_steps"], 4, t)
                hop(step, "hop1", t, b)
                step(nc.vector.tensor_scalar(tt(t), post[:], d(t, 1), None, ALU.mult))
                dve.sem_inc(S["hop1", "table_ready"], 1)
                step.close()

            def hop2_rows(t, b):
                n = "hop2"
                step = Steps(dve, S[n, "dve_steps"], 3, t)
                hop(step, n, t, b)
                step(nc.vector.tensor_scalar(post[:], post[:], 0.0, None, ALU.max))
                dve.sem_inc(S[n, "rows_ready"], 1)
                step.close()

            def hop2_product(t, b):
                n = "hop2"
                step = Steps(dve, S[n, "dve_steps2"], 6, t)
                step(nc.vector.tensor_tensor(xt(t), xt(t), hopb_sb[:], ALU.add))
                dve.wait_ge(S[n, "product_ready"], t + 1)
                step(nc.vector.tensor_tensor(xt(t), prod[:, 0:D], xt(t), ALU.add))
                normed_free(n, t)
                norm(n, step, xt(t), normed[:])
                dve.sem_inc(S[n, "normed_ready"], 1)
                step.close()

            def rel1_rows(t, b):
                n = "rel1"
                step = Steps(dve, S[n, "dve_steps"], 1, t)
                dve.wait_ge(agg_ready, t + (before(n) * TILES + 1))
                rows_free(n, t)
                step(nc.vector.tensor_copy(post[:], agg[b][:, 0:D]))
                dve.sem_inc(agg_free, 1)
                dve.sem_inc(S[n, "rows_ready"], 1)
                step.close()

            def rel2_rows(t, b):
                n = "rel2"
                step = Steps(dve, S[n, "dve_steps"], 1, t)
                dve.wait_ge(agg_ready, t + (before(n) * TILES + 1))
                step(nc.vector.tensor_tensor(xt(t), agg[b][:, 0:D], xt(t), ALU.add))
                dve.sem_inc(agg_free, 1)
                dve.sem_inc(S[n, "table_ready"], 1)
                step.close()

            parts = {
                "sage": [(2, sage_product), (1, sage_rows), (3, sage_table)],
                "gcn1": [(1, gcn1_rows)],
                "gcn2": [(2, gcn2_product), (1, gcn2_rows)],
                "hop1": [(1, hop1_rows)],
                "hop2": [(2, hop2_product), (1, hop2_rows), (3, lambda t, b: relations("hop2", t))],
                "rel1": [(1, rel1_rows), (1, lambda t, b: relations("rel1", t))],
                "rel2": [(1, rel2_rows)],
            }
            for n in NAMES:
                if n in ("hop2", "rel1"):
                    dve.wait_ge(s_wrel[0 if n == "hop2" else 1], 16 * (KB + 2))
                over_tiles(dve, visits_of(n), parts[n])


_INS = ["x", "src", "dst", "edge_type_8", "edge_weight", "L0_gnn_w_self", "L0_gnn_w_neigh", "L1_gnn_W1",
        "L1_gnn_b1", "L1_gnn_W2", "L1_gnn_b2", "L2_gnn_W", "L2_gnn_b", "L3_gnn_W0", "L3_gnn_b0",
        "L3_gnn_W1", "L3_gnn_b1"]


def kernel(**inputs):
    import concourse.bacc as bacc
    from concourse.bass_utils import run_bass_kernel_spmd

    nc = bacc.Bacc("TRN2", target_bir_lowering=False, num_devices=1)
    arrays, args = {}, []
    for name in _INS:
        a = np.ascontiguousarray(inputs[name])
        arrays[f"in_{name}"] = a
        args.append(nc.dram_tensor(f"in_{name}", a.shape, mybir.dt.from_np(a.dtype), kind="ExternalInput").ap())
    shape = inputs["x"].shape
    args.append(nc.dram_tensor("out_x", shape, F32, kind="ExternalOutput").ap())
    build_gnn(nc, *args)
    result = run_bass_kernel_spmd(nc, [arrays], core_ids=[0])
    return result.results[0]["out_x"]
```

```python
from contextlib import ExitStack

import numpy as np

import concourse.bass as bass
from concourse import mybir

F32 = mybir.dt.float32
BF16 = mybir.dt.bfloat16
I32 = mybir.dt.int32
U32 = mybir.dt.uint32
ALU = mybir.AluOpType
ACT = mybir.ActivationFunctionType
AXX = mybir.AxisListType.X

P = 128
LN_EPS = 1e-5
NORM_EPS = 1e-12
DEG_EPS = 1e-12
PAD_DST = 4095.0


class Steps:

    def __init__(self, eng, sem, per, t):
        self.eng, self.sem, self.per, self.t, self.k = eng, sem, per, t, 0

    def __call__(self, ins):
        self.k += 1
        ins.then_inc(self.sem, 1)
        self.eng.wait_ge(self.sem, self.t * self.per + self.k)

    def close(self):
        assert self.k == self.per, (self.k, self.per)


def build_gnn(nc, x, src, dst, edge_type, edge_weight, w_self, w_neigh, gcn_w1, gcn_b1, gcn_w2,
              gcn_b2, hop_w, hop_b, rel_w0, rel_b0, rel_w1, rel_b1, out):
    N, D = x.shape
    E = src.shape[0]
    HID = gcn_w1.shape[1]
    REL = rel_w0.shape[0]
    TILES = -(-N // P)
    LAST = N - (TILES - 1) * P
    NPAD = TILES * P
    CHUNKS = -(-E // P)
    QUAD = 4
    QUADS = CHUNKS // QUAD
    VISITS = QUADS + TILES - 1
    KB = D // P
    BUCKETS = TILES + 1
    QP, QB = 104, 4
    GRING = 32
    GQ = GRING // QUAD
    STAGE = 16
    BLOCKS = CHUNKS // STAGE
    ROUNDS = CHUNKS // GRING
    BOUNDS = P - 1
    TSHIFT = 7
    assert QP * QB == CHUNKS and CHUNKS % GRING == 0 and GRING == 2 * STAGE
    assert D == 256 and HID == P and E < CHUNKS * P and 1 << TSHIFT == P
    LOADED = [(lo, min(lo + 8, TILES - 1)) for lo in range(0, TILES - 1, 8)] + [(TILES - 1, TILES)]
    NORMED = LOADED[:-2] + [(LOADED[-2][0], TILES)]
    STORED = [(lo, min(lo + 4, TILES)) for lo in range(0, TILES, 4)]
    TAIL = E - (CHUNKS - 1) * P

    PASSES = {"sage": (True, D), "gcn1": (False, HID), "gcn2": (False, HID), "hop1": (True, D),
              "hop2": (True, D), "rel1": (False, D), "rel2": (False, D)}
    NAMES = list(PASSES)

    with ExitStack() as ctx:
        def sb(name, shape, dt=F32):
            return ctx.enter_context(nc.sbuf_tensor(name, shape, dt))

        def psum(name, shape):
            return ctx.enter_context(nc.psum_tensor(name, shape, F32))

        def sem(name):
            return ctx.enter_context(nc.semaphore(name))

        def dram(name, shape):
            return nc.dram_tensor(name, shape, F32).ap()

        tables = {n: dram(f"table_{n}", (NPAD, PASSES[n][1])) for n in NAMES[:5]}
        tables["rel1"] = dram("table_rel1", (REL * NPAD, D))
        tables["rel2"] = dram("table_rel2", (REL * NPAD, D))
        sorted_dram = dram("edges_sorted", (CHUNKS * P, 4))

        x_sb = sb("x_sb", [P, TILES * D])
        h_sb = sb("h_sb", [P, TILES * D])
        t_sb = sb("t_sb", [P, TILES * D])
        gathered = sb("gathered", [P, GRING * D])
        onehot = sb("onehot", [P, 2 * QUAD, P])
        onehot1 = sb("onehot1", [P, 2 * QUAD, P], BF16)
        iota = sb("iota", [P, NPAD])
        edges = sb("edges", [P, CHUNKS, 4])
        one_w = sb("one_w", [P, CHUNKS, 4], BF16)
        idx_node = sb("idx_node", [P, CHUNKS], U32)
        idx_rel = sb("idx_rel", [P, CHUNKS], U32)
        stage_idx = sb("stage_idx", [P, 2, STAGE], U32)
        stage_rec = sb("stage_rec", [P, STAGE * 4])
        bounds = sb("bounds", [P, TILES + 1], I32)
        dinv = sb("dinv", [P, TILES, 2])
        hdinv = sb("hdinv", [P, TILES])
        ident = sb("ident", [P, P])
        lower = sb("lower", [P, P])
        ones = sb("ones", [P, P])
        eps = sb("eps", [P, 1])
        wself_t = sb("wself_t", [P, KB, D])
        wneigh_t = sb("wneigh_t", [P, KB, D])
        hopw_t = sb("hopw_t", [P, KB, D])
        w1_sb = sb("w1_sb", [P, KB, HID])
        w2_sb = sb("w2_sb", [P, D])
        relw = sb("relw", [P, KB, REL, D])
        y_sb = sb("y_sb", [P, REL, D])
        b1_sb = sb("b1_sb", [P, HID])
        b2_sb = sb("b2_sb", [P, D])
        hopb_sb = sb("hopb_sb", [P, D])
        relb_sb = sb("relb_sb", [P, 2, D])
        post = sb("post", [P, D + 4])
        post2 = sb("post2", [P, D])
        turned = sb("turned", [P, 2 * KB, P])
        normed = sb("normed", [P, 2, D])
        normed_t = sb("normed_t", [P, KB, P])
        small = sb("small", [P, 2, 24])
        bnst = sb("bnst", [P, 6])
        bn_all = sb("bn_all", [P, TILES, 6])
        mv_all = sb("mv_all", [P, TILES, 2])
        rstd_all = sb("rstd_all", [P, TILES])
        shift_all = sb("shift_all", [P, TILES])
        flag = sb("flag", [P, 1], I32)
        post2n = sb("post2n", [P, D])

        F = QB * P
        flat_i = gathered[0:QP, 0:3 * F].bitcast(I32)
        flat_w = gathered[0:QP, 3 * F:4 * F]
        flat_next = gathered[0:QP, 4 * F:5 * F].bitcast(I32)
        flat_f = gathered[0:QP, 5 * F:9 * F]
        flat_s = gathered[0:QP, 9 * F:13 * F]
        drop = gathered[0:QP, 13 * F:14 * F]
        free = [0]

        def scratch(n):
            free[0] += n
            assert free[0] <= TILES * D
            return t_sb[:, free[0] - n:free[0]]

        wraw = scratch(3 * KB * D)
        tile_f, mask, pos, rest_w, rest_w2 = (scratch(CHUNKS) for _ in range(5))
        tile_i = scratch(CHUNKS).bitcast(I32)
        pos_u = scratch(CHUNKS).bitcast(U32)
        scans = scratch(2 * (256 + CHUNKS))
        scan = [scans[:, k * (256 + CHUNKS):(k + 1) * (256 + CHUNKS)] for k in range(2)]
        within = scans.bitcast(BF16)[:, 0:TILES * QUADS].rearrange("p (t q) -> p t q", t=TILES)
        tot, base, totals = (scratch(32)[:, 0:BUCKETS] for _ in range(3))
        ends = [scratch(32 + BUCKETS) for _ in range(2)]
        groups = scratch(32)[:, 0:TILES]
        drops = scratch(2)

        agg = [psum("agg0", [P, 512]), psum("agg1", [P, 512])]
        turn_ps = psum("turn_ps", [P, 2 * KB, P])
        prod = psum("prod", [P, 512])
        y_ps = [psum(f"y{g}", [P, 2, D]) for g in range(REL // 2)]
        prod2 = y_ps[3][:].rearrange("p a b -> p (a b)")
        normed_ps = {"sage": y_ps[0][:].rearrange("p a (b c) -> p (a b) c", c=P), "hop2": turn_ps}

        s_x = [sem(f"x_loaded{k}") for k in range(len(LOADED))]
        s_edge = sem("edges_loaded")
        s_w = sem("weights_loaded")
        s_wrel = [sem("rel_w0_loaded"), sem("rel_w1_loaded")]
        s_fill = sem("memory_filled")
        s_pad = sem("padding_ready")
        s_const = sem("constants_made")
        s_prep = sem("prep_dve_steps")
        s_flat = sem("flat_fields_ready")
        s_flat_t = sem("flat_fields_turned")
        s_edgef = sem("edge_fields_copied")
        s_tot = sem("bucket_totals_ready")
        s_totmm = sem("bucket_offsets_ready")
        s_pos = sem("positions_ready")
        s_stage = [sem(f"index_stage_filled{h}") for h in range(2)]
        s_total_steps = sem("total_steps")
        s_rank = sem("rank_steps")
        s_idx = sem("indices_ready")
        s_wt = sem("weight_turned")
        s_wtc = sem("weight_turned_copied")
        s_bn = sem("first_norm_stats")
        s_mv = sem("first_norm_variances")
        s_std = sem("first_norm_roots")
        s_warm = sem("roots_warmed_up")
        s_rstd = sem("first_norm_scales")
        s_scaled = sem("first_norm_scaled")
        s_drops = sem("drops_counted")
        s_dropmm = sem("drops_summed")
        s_flag = sem("flag_ready")
        s_scat = sem("records_scattered")
        s_scat_stage = sem("scatter_stage_filled")
        s_sort_prep = sem("sort_prep_steps")
        s_sort = sem("sort_steps")
        s_bounds = sem("bounds_ready")
        s_weights = sem("weights_split")
        s_srt = sem("sorted_reloaded")
        s_out = sem("out_stored")
        s_passed = [sem("pool_wait_passed"), sem("dve_wait_passed")]
        s_land = [sem(f"place_landed{k}") for k in range(GQ)]

        quad_landed = sem("quad_landed")
        quad_free = sem("quad_free")
        onehot_ready = sem("onehot_ready")
        pair_free = sem("pair_free")
        agg_ready = sem("agg_ready")
        agg_free = sem("agg_free")

        def before(n):
            return NAMES.index(n)

        pair_stored = [sem(f"relation_pair_stored{g}") for g in range(REL // 2)]

        S = {}
        for n in NAMES:
            for what in ("table_ready", "table_stored", "dve_steps"):
                if what != "table_stored" or n not in ("rel1", "rel2"):
                    S[n, what] = sem(f"{n}_{what}")
        norm = ("var_ready", "std_ready")
        product = ("rows_ready", "rows_turned", "turned_copied", "product_ready", "product_free", "dve_steps2")
        second = ("normed_ready", "normed_turned", "normed_copied")
        ys = ("y_ready", "y_added", "y_in_sbuf")
        for n, names in {"sage": product + norm + second + ("self_copied", "square_ready", "length_ready",
                                                            "degree_ready", "degree_root", "product2_ready",
                                                            "product2_free"),
                         "gcn2": product + norm, "hop2": product + norm + second + ys,
                         "rel1": product + ys}.items():
            for what in names:
                S[n, what] = sem(f"{n}_{what}")

        block = ctx.enter_context(nc.Block())

        def xt(t):
            return x_sb[:, bass.ds(t * D, D)]

        def ht(t):
            return h_sb[:, bass.ds(t * D, D)]

        def tt(t, w=D):
            return t_sb[:, bass.ds(t * D, w)]

        def bounds_of(eng, t):
            first = eng.value_load(bounds[BOUNDS:P, bass.ds(t, 1)], min_val=0, max_val=QUADS - 1)
            last = eng.value_load(bounds[BOUNDS:P, bass.ds(t + 1, 1)], min_val=0, max_val=QUADS - 1)
            return first, last

        def over_tiles(eng, visits, parts, ending=None, early=False):
            most = max([lag for lag, _ in parts], default=0)
            start = most + (TILES - 1 - most) % 2

            def behind(tile, bank, known):
                for lag, part in parts:
                    if known is None or 0 <= known - lag < TILES:
                        part(tile(lag), (bank - lag) % 2)

            def round_(tile, bank, known=None):
                if early:
                    limits = bounds_of(eng, tile(-1))
                behind(tile, bank, known)
                if visits:
                    visits(tile(-1), (bank + 1) % 2, limits if early else bounds_of(eng, tile(-1)))

            if visits:
                visits(0, 0, bounds_of(eng, 0))
            for i in range(start):
                round_(lambda lag, i=i: i - lag, i % 2, i)
            with eng.Fori(0, (TILES - 1 - start) // 2) as j:
                for k in range(2):
                    round_(lambda lag, k=k: j * 2 + (start + k - lag), (start + k) % 2)
            behind(lambda lag: TILES - 1 - lag, (TILES - 1) % 2, TILES - 1)
            for back, part in ending or ():
                part(TILES - back, (TILES - back) % 2)
            for i in range(TILES, TILES + most if ending is None else 0):
                behind(lambda lag, i=i: i - lag, i % 2, i)

        def relation_rows(n, t):
            last = TILES - (4 if n == "hop2" else 2)
            if isinstance(t, int) and t >= last:
                place = gathered[:, (t - last) * REL * D:(t - last + 1) * REL * D]
                return place.rearrange("p (r d) -> p r d", d=D), False
            return y_sb, True

        def out_of_order(eng):
            return eng.value_load(flag[0:1, 0:1], min_val=0, max_val=CHUNKS * P)

        @block.sync
        def _(sp):
            for k, (lo, hi) in enumerate(LOADED[:-1]):
                sp.dma_start(x_sb[:, lo * D:hi * D].rearrange("p (t d) -> p t d", d=D),
                             x[lo * P:hi * P].rearrange("(t p) d -> p t d", p=P)).then_inc(s_x[k], 16)
            sp.wait_ge(s_pad, 1)
            sp.dma_start(x_sb[0:LAST, (TILES - 1) * D:TILES * D], x[(TILES - 1) * P:N]
                         ).then_inc(s_x[-1], 16)
            sp.wait_ge(s_edge, 16 * 15)
            for k, w in enumerate((w_self, w_neigh, hop_w)):
                sp.dma_start(wraw[:, k * KB * D:(k + 1) * KB * D].rearrange("p (m i) -> p m i", m=KB),
                             w.rearrange("(m p) i -> p m i", p=P)).then_inc(s_w, 16)
            for lo, hi in STORED:
                sp.wait_ge(s_scaled, hi)
                sp.dma_start(tables["sage"].rearrange("(t p) d -> p t d", p=P)[:, lo:hi, :],
                             h_sb[:, lo * D:hi * D].rearrange("p (t d) -> p t d", d=D)
                             ).then_inc(S["sage", "table_stored"], 16)
            sp.wait_ge(s_flag, 1)
            with sp.If(out_of_order(sp) > 0):
                sp.wait_ge(s_scat, 16 * CHUNKS)
                for b in range(QB):
                    sp.dma_start(flat_s[:, b * 4 * P:(b + 1) * 4 * P],
                                 sorted_dram[b * QP * P:(b + 1) * QP * P].rearrange("(q e) f -> q (e f)", q=QP)
                                 ).then_inc(s_srt, 16)

            def stage(index, at, h):
                sp.dma_start(stage_idx[:, h, :], index[:, bass.ds(at, STAGE)]).then_inc(s_stage[h], 16)

            sp.wait_ge(s_idx, 2)
            for h in range(2):
                stage(idx_node, h * STAGE, h)

            sp.dma_start(w1_sb[:], gcn_w1.rearrange("(k p) o -> p k o", p=P)).then_inc(s_w, 16)
            sp.dma_start(w2_sb[:], gcn_w2).then_inc(s_w, 16)
            sp.dma_start(b1_sb[:], gcn_b1.partition_broadcast(P)).then_inc(s_w, 16)
            sp.dma_start(b2_sb[:], gcn_b2.partition_broadcast(P)).then_inc(s_w, 16)
            sp.dma_start(hopb_sb[:], hop_b.partition_broadcast(P)).then_inc(s_w, 16)

            def load_relations(w, b, s):
                for j in range(2):
                    sp.dma_start(relb_sb[:, j, :], b.partition_broadcast(P)).then_inc(s, 16)
                for k in range(KB):
                    sp.dma_start(relw[:, k, :, :], w[:, k * P:(k + 1) * P, :].rearrange("r p o -> p r o")
                                 ).then_inc(s, 16)

            load_relations(rel_w0, rel_b0, s_wrel[0])

            for pi, n in enumerate(NAMES):
                if n == "rel1":
                    for g in range(REL // 2):
                        sp.wait_ge(pair_stored[g], 16 * TILES + 1)
                    load_relations(rel_w1, rel_b1, s_wrel[1])
                index = idx_rel if n in ("rel1", "rel2") else idx_node
                index2 = idx_rel if n in ("hop2", "rel1") else idx_node

                def land(r, h):
                    for k in range(h * GQ // 2, (h + 1) * GQ // 2):
                        sp.wait_ge(s_land[k], (r + (1 + pi * ROUNDS)) * (16 * QUAD))
                        sp.sem_inc(quad_landed, 1)

                with sp.Fori(0, ROUNDS - 1) as r:
                    for h in range(2):
                        land(r, h)
                        stage(index, (r + 1) * GRING + h * STAGE, h)
                for h in range(2):
                    land(ROUNDS - 1, h)
                    if pi < len(NAMES) - 1:
                        stage(index2, h * STAGE, h)
            sp.wait_ge(s_out, 16 * TILES)

        @block.gpsimd
        def _(pool):
            nc.gpsimd.memset(flat_i[:, 0:QB * P], 0).then_inc(s_fill, 1)
            nc.gpsimd.memset(flat_i[:, QB * P:2 * QB * P], int(PAD_DST)).then_inc(s_fill, 1)
            nc.gpsimd.memset(flat_i[:, 2 * QB * P:3 * QB * P], 0).then_inc(s_fill, 1)
            nc.gpsimd.memset(flat_w, 0.0).then_inc(s_fill, 1)
            nc.gpsimd.memset(flat_next, int(PAD_DST)).then_inc(s_fill, 1)
            nc.gpsimd.memset(x_sb[:, (TILES - 1) * D:TILES * D], 0.0).then_inc(s_fill, 1)
            pool.wait_ge(s_fill, 6)
            pool.sem_inc(s_pad, 1)
            nc.gpsimd.iota(iota[:], pattern=[[1, NPAD]], base=0, channel_multiplier=0,
                           allow_small_or_imprecise_dtypes=True).then_inc(s_const, 1)
            nc.gpsimd.memset(ident[:], 0.0).then_inc(s_fill, 1)
            nc.gpsimd.memset(lower[:], 0.0).then_inc(s_fill, 1)
            pool.wait_ge(s_fill, 8)
            nc.gpsimd.affine_select(out=ident[:], in_=ident[:], compare_op=ALU.not_equal, fill=1.0,
                                    base=0, pattern=[[-1, P]], channel_multiplier=1).then_inc(s_const, 1)
            nc.gpsimd.affine_select(out=lower[:], in_=lower[:], compare_op=ALU.is_ge, fill=1.0,
                                    base=0, pattern=[[-1, P]], channel_multiplier=1).then_inc(s_const, 1)
            nc.gpsimd.memset(ones[:], 1.0).then_inc(s_const, 1)
            nc.gpsimd.memset(eps[:], LN_EPS).then_inc(s_const, 1)

            pool.wait_ge(s_flag, 1)
            with pool.If(out_of_order(pool) > 0):
                pool.wait_ge(s_pos, 1)
                with pool.Fori(0, BLOCKS) as r:
                    nc.gpsimd.tensor_copy(stage_idx[:, 0, :], pos_u[:, bass.ds(r * STAGE, STAGE)]
                                          ).then_inc(s_scat_stage, 1)
                    nc.gpsimd.tensor_copy(stage_rec[:].rearrange("p (c f) -> p c f", f=4),
                                          edges[:, bass.ds(r * STAGE, STAGE), :]).then_inc(s_scat_stage, 1)
                    pool.wait_ge(s_scat_stage, r * 2 + 2)
                    pool.sem_inc(s_passed[0], 1)
                    for k in range(STAGE):
                        pool.indirect_dma_start(
                            sorted_dram, bass.IndirectOffsetOnAxis(ap=stage_idx[:, 0, k:k + 1], axis=0),
                            stage_rec[:, k * 4:(k + 1) * 4], None).then_inc(s_scat, 16)
                    pool.wait_ge(s_scat, r * (16 * STAGE) + 16 * STAGE)

            pool.wait_ge(s_idx, 2)
            for pi, n in enumerate(NAMES):
                width = PASSES[n][1]
                if n in ("rel1", "rel2"):
                    for g in range(REL // 2):
                        pool.wait_ge(pair_stored[g], 16 * TILES * (1 if n == "rel1" else 2) + 1)
                else:
                    pool.wait_ge(S[n, "table_stored"], 16 * len(STORED) if n == "sage" else 16 * TILES + 1)
                with pool.Fori(0, ROUNDS) as r:
                    for h in range(2):
                        pool.wait_ge(s_stage[h], (r + (pi * ROUNDS + 1)) * 16)
                        pool.sem_inc(s_passed[0], 1)
                        for k in range(STAGE):
                            slot = h * STAGE + k
                            if k % QUAD == 0:
                                pool.wait_ge(quad_free, r * GQ + (pi * (QUADS - 1) + slot // QUAD + 1))
                                pool.sem_inc(s_passed[0], 1)
                            pool.indirect_dma_start(
                                gathered[:, slot * D:slot * D + width], None, tables[n],
                                bass.IndirectOffsetOnAxis(ap=stage_idx[:, h, k:k + 1], axis=0)
                            ).then_inc(s_land[slot // QUAD], 16)

        def over_groups(eng, lo, hi, group):
            group(lo, 0, first=True)
            with eng.If(lo + 1 < hi):
                with eng.Fori(lo + 1, hi, 2) as q:
                    group(q, 1)
                    group(q + 1, 0)
            with eng.If(((hi + lo) & 1) > 0):
                group(hi, 1)

        @block.tensor
        def _(pe):
            pe.sem_inc(pair_free, 4)
            pe.sem_inc(agg_free, 2)
            pe.wait_ge(s_const, 5)

            def turn_edges(rows, first):
                for b in range(QB):
                    if first + b >= 2:
                        pe.wait_ge(s_edgef, first + b - 1)
                    for f in range(4):
                        mm = pe.transpose(y_ps[b % 2][0:P, f // 2, (f % 2) * P:(f % 2) * P + QP],
                                          rows(b, f), ident[0:QP, 0:QP])
                    mm.then_inc(s_flat_t, 1)

            pe.wait_ge(s_drops, 1)
            pe.matmul(prod2[:, 0:1], ones[0:QP, :], drops[0:QP, 0:1], start=True, stop=True).then_inc(s_dropmm, 1)
            pe.wait_ge(s_flat, 1)
            turn_edges(lambda b, f: flat_f[:, (f * QB + b) * P:(f * QB + b + 1) * P], 0)

            pe.wait_ge(s_flag, 1)
            with pe.If(out_of_order(pe) > 0):
                pe.wait_ge(s_tot, 1)
                pe.matmul(prod[:, 0:BUCKETS], ones[:], tot, start=True, stop=True)
                pe.matmul(prod[:, 64:64 + BUCKETS], lower[:], tot, start=True, stop=True).then_inc(s_totmm, 1)
                pe.wait_ge(s_srt, 16 * QB)
                turn_edges(lambda b, f: flat_s[:, b * 4 * P:(b + 1) * 4 * P].rearrange("q (e f) -> q f e", f=4)[:, f, :],
                           QB)

            pe.wait_ge(s_edgef, QB)
            pe.sem_inc(quad_free, GQ)

            pe.wait_ge(s_w, 16 * 8)
            for k in range(3):
                if k >= 1:
                    pe.wait_ge(s_wtc, k)
                for m in range(KB):
                    for j in range(KB):
                        mm = pe.transpose(turn_ps[:, j * KB + m, :],
                                          wraw[:, (k * KB + m) * D + j * P:(k * KB + m) * D + (j + 1) * P], ident[:])
                mm.then_inc(s_wt, 1)
            pe.wait_ge(s_wtc, 3)
            pe.wait_ge(s_bounds, 1)
            pe.wait_ge(s_weights, 1)

            def visits_of(n):
                width = PASSES[n][1]
                quads0, made0, tiles0 = before(n) * QUADS, before(n) * 2 * VISITS, before(n) * TILES

                def group(q, t, b, half, first=False):
                    u = q + t
                    pe.wait_ge(quad_landed, q + (quads0 + 1))
                    for k in range(QUAD):
                        if k % 2 == 0:
                            pe.wait_ge(onehot_ready, u * 2 + (made0 + k // 2 + 1))
                        mm = pe.matmul(agg[b][:, 0:width], onehot[:, half * QUAD + k, :],
                                       gathered[:, bass.ds((q & (GQ - 1)) * (QUAD * D) + k * D, width)],
                                       start=first and k == 0, stop=True, skip_group_check=True)
                        if n == "sage":
                            mm = pe.matmul(agg[b][:, D:D + 4], onehot1[:, half * QUAD + k, :],
                                           one_w[:, bass.ds(q * QUAD + k, 1), :].rearrange("p c k -> p (c k)"),
                                           start=False, stop=True, skip_group_check=True)
                        if k % 2 == 1:
                            mm.then_inc(pair_free, 1)
                        elif k == 0 and not first:
                            mm.then_inc(quad_free, 1)

                def visits(t, b, limits):
                    lo, hi = limits
                    pe.wait_ge(agg_free, t + (tiles0 + 1))
                    over_groups(pe, lo, hi, lambda q, half, first=False: group(q, t, b, half, first))
                    pe.drain().then_inc(agg_ready, 1)
                return visits

            def turn(n, rows, t):
                pe.wait_ge(S[n, "rows_ready"], t + 1)
                for k, r in enumerate(rows):
                    mm = pe.transpose(turn_ps[:, k, :], r, ident[:])
                mm.then_inc(S[n, "rows_turned"], 1)

            def turn_normed(n, t, b):
                pe.wait_ge(S[n, "normed_ready"], t + 1)
                if n == "hop2":
                    pe.wait_ge(S[n, "turned_copied"], min(t + 2, TILES) if isinstance(t, int) else t + 2)
                for k in range(KB):
                    mm = pe.transpose(normed_ps[n][:, k, :], normed[:, b, k * P:(k + 1) * P], ident[:])
                mm.then_inc(S[n, "normed_turned"], 1)

            def product(to, rows_t, blocks, done):
                for k, w in enumerate(blocks):
                    mm = pe.matmul(to, rows_t[:, k, :], w, start=(k == 0), stop=(k == len(blocks) - 1))
                mm.then_inc(done, 1)

            def relations(n, rows_t, t):
                for g in range(REL // 2):
                    pe.wait_ge(S[n, "y_added"], t * (REL // 2) + (g + 1))
                    for k in range(KB):
                        mm = pe.matmul(y_ps[g][:], rows_t[:, k, :], relw[:, k, 2 * g:2 * g + 2, :],
                                       start=(k == 0), stop=(k == KB - 1))
                    mm.then_inc(S[n, "y_ready"], 1)

            halves = [post[:, k * P:(k + 1) * P] for k in range(KB)]
            selfs = [post2[:, k * P:(k + 1) * P] for k in range(KB)]

            def sage_turn(t, b):
                pe.wait_ge(S["sage", "self_copied"], t + 1)
                turn("sage", halves + selfs, t)

            def sage_table(t, b):
                pe.wait_ge(S["sage", "normed_copied"], t + 1)
                pe.wait_ge(S["sage", "product2_free"], t + 1)
                product(prod2[:, 0:HID], normed_t, [w1_sb[:, k, :] for k in range(KB)],
                        S["sage", "product2_ready"])

            def rows_product(n, blocks):
                def part(t, b):
                    pe.wait_ge(S[n, "turned_copied"], t + 1)
                    pe.wait_ge(S[n, "product_free"], t + 1)
                    product(prod[:, 0:D], turned, blocks, S[n, "product_ready"])
                return part

            def hop2_turn(t, b):
                pe.wait_ge(S["hop2", "normed_copied"], t + 1)
                turn("hop2", halves, t)

            def hop2_relations(t, b):
                pe.wait_ge(S["hop2", "normed_copied"], t + 3)
                relations("hop2", normed_t, t)

            def rel1_relations(t, b):
                pe.wait_ge(S["rel1", "turned_copied"], t + 1)
                relations("rel1", turned, t)

            def columns(*weights):
                return [w[:, k, :] for w in weights for k in range(KB)]

            parts = {"sage": [(1, sage_turn), (3, sage_table), (1, rows_product("sage", columns(wneigh_t, wself_t))),
                              (2, lambda t, b: turn_normed("sage", t, b))],
                     "gcn1": [],
                     "gcn2": [(1, lambda t, b: turn("gcn2", halves[0:1], t)), (1, rows_product("gcn2", [w2_sb[:]]))],
                     "hop1": [],
                     "hop2": [(1, hop2_turn), (3, hop2_relations), (2, lambda t, b: turn_normed("hop2", t, b)),
                              (1, rows_product("hop2", columns(hopw_t)))],
                     "rel1": [(1, lambda t, b: turn("rel1", halves, t)), (1, rel1_relations)],
                     "rel2": []}
            for n in NAMES:
                if n in ("hop2", "rel1"):
                    pe.sem_inc(S[n, "y_added"], REL // 2)
                    pe.wait_ge(s_wrel[0 if n == "hop2" else 1], 16 * (KB + 2))
                if n == "sage":
                    pe.sem_inc(S[n, "product2_free"], 1)
                if n in ("sage", "gcn2", "hop2"):
                    pe.sem_inc(S[n, "product_free"], 1)
                if n in ("sage", "gcn2", "hop2", "rel1"):
                    pe.sem_inc(S[n, "rows_turned"], 1)
                if n == "hop2":
                    pe.sem_inc(S[n, "normed_copied"], 2)
                if n in ("sage", "hop2"):
                    pe.sem_inc(S[n, "normed_turned"], 2)
                over_tiles(pe, visits_of(n), parts[n])

        @block.scalar
        def _(act):
            act.wait_ge(s_pad, 1)
            full = (CHUNKS - QP) * P
            for a, to, off in ((dst, flat_i[:, F:2 * F], 0), (dst, flat_next, 1), (src, flat_i[:, 0:F], 0),
                               (edge_type, flat_i[:, 2 * F:3 * F], 0), (edge_weight, flat_w, 0)):
                act.dma_start(to[:, 0:F - P].rearrange("q (b e) -> q b e", e=P),
                              a[off:off + full].rearrange("(b q e) -> q b e", q=QP, e=P)).then_inc(s_edge, 16)
                act.dma_start(to[0:QP - 1, F - P:F],
                              a[off + full:off + full + (QP - 1) * P].rearrange("(q e) -> q e", e=P)
                              ).then_inc(s_edge, 16)
                act.dma_start(to[QP - 1:QP, F - P:F - P + TAIL - off],
                              a[off + full + (QP - 1) * P:E].rearrange("(q e) -> q e", q=1)).then_inc(s_edge, 16)

            act.wait_ge(s_const, 5)
            nc.scalar.activation(small[:, 0, 20:21], eps[:], ACT.Sqrt).then_inc(s_warm, 1)
            for k, (lo, hi) in enumerate(NORMED):
                act.wait_ge(s_mv, hi)
                nc.scalar.activation(rstd_all[:, lo:hi], mv_all[:, lo:hi, 1], ACT.Sqrt, bias=eps[:]).then_inc(s_std, 1)
                act.wait_ge(s_rstd, 2 * (k + 1))
                for t in range(lo, hi):
                    nc.scalar.activation(ht(t), xt(t), ACT.Relu, scale=rstd_all[:, t:t + 1],
                                         bias=shift_all[:, t:t + 1]).then_inc(s_scaled, 1)
            for k, w in enumerate((wself_t, wneigh_t, hopw_t)):
                act.wait_ge(s_wt, k + 1)
                nc.scalar.copy(w[:].rearrange("p k o -> p (k o)"),
                               turn_ps[:].rearrange("p k o -> p (k o)")).then_inc(s_wtc, 1)
            for n in NAMES[1:5]:
                act.sem_inc(S[n, "table_stored"], 1)
            for g in range(REL // 2):
                act.sem_inc(pair_stored[g], 1)

            def copy_turned(n, blocks, t):
                act.wait_ge(S[n, "rows_turned"], t + 2)
                nc.scalar.copy(turned[:, 0:blocks, :].rearrange("p k o -> p (k o)"),
                               turn_ps[:, 0:blocks, :].rearrange("p k o -> p (k o)")
                               ).then_inc(S[n, "turned_copied"], 1)

            def copy_normed(n, t):
                act.wait_ge(S[n, "normed_turned"], t + 3)
                nc.scalar.copy(normed_t[:], normed_ps[n][:, 0:KB, :]).then_inc(S[n, "normed_copied"], 1)

            def root(n, t):
                act.wait_ge(S[n, "var_ready"], t + 1)
                nc.scalar.activation(small[:, 0, 2:3], small[:, 0, 1:2], ACT.Sqrt, bias=eps[:]
                                     ).then_inc(S[n, "std_ready"], 1)

            def store(n, to, t):
                act.wait_ge(S[n, "table_ready"], t + 1)
                act.dma_start(tables[to][bass.ds(t * P, P), :], tt(t, PASSES[to][1])
                              ).then_inc(S[to, "table_stored"], 16)

            def finish_relations(n, to, t):
                rows, _ = relation_rows(n, t)
                for g in range(REL // 2):
                    act.wait_ge(S[n, "y_added"], t * (REL // 2) + (REL // 2 + g + 1))
                    pair = rows[:, 2 * g:2 * g + 2, :]
                    nc.scalar.activation(pair, pair, ACT.Relu).then_inc(S[n, "y_in_sbuf"], 1)
                    act.wait_ge(S[n, "y_in_sbuf"], t * (REL // 2) + (g + 1))
                    act.dma_start(tables[to].rearrange("(r n) d -> n r d", r=REL)[bass.ds(t * P, P), 2 * g:2 * g + 2, :],
                                  pair).then_inc(pair_stored[g], 16)

            def sage_rows(t, b):
                n = "sage"
                act.wait_ge(agg_ready, t + (before(n) * TILES + 1))
                act.wait_ge(S[n, "rows_turned"], t + 1)
                nc.scalar.copy(post[:], agg[b][:, 0:D + 4]).then_inc(S[n, "rows_ready"], 1)
                act.wait_ge(S[n, "rows_ready"], t + 1)
                act.sem_inc(agg_free, 1)
                nc.scalar.copy(post2[:], ht(t)).then_inc(S[n, "self_copied"], 1)

            def sage_degree_root(t, b):
                n = "sage"
                act.wait_ge(S[n, "degree_ready"], t + 1)
                nc.scalar.activation(small[:, b, 10:12], small[:, b, 8:10], ACT.Sqrt).then_inc(S[n, "degree_root"], 1)

            def sage_table(t, b):
                n = "sage"
                act.wait_ge(S[n, "product2_ready"], t + 1)
                nc.scalar.activation(tt(t, HID), prod2[:, 0:HID], ACT.Copy,
                                     scale=dinv[:, bass.ds(t, 1), 0:1].rearrange("p a b -> p (a b)")
                                     ).then_inc(S[n, "table_ready"], 1)
                store(n, "gcn1", t)
                act.sem_inc(S[n, "product2_free"], 1)

            def sage_length(t, b):
                n = "sage"
                act.wait_ge(S[n, "product_ready"], t + 1)
                nc.scalar.activation(y_sb[:, 0, :], prod[:, 0:D], ACT.Square, accum_out=small[:, b, 4:5]
                                     ).then_inc(S[n, "square_ready"], 1)
                act.wait_ge(S[n, "square_ready"], t + 1)
                nc.scalar.activation(small[:, b, 5:6], small[:, b, 4:5], ACT.Sqrt).then_inc(S[n, "length_ready"], 1)

            parts = {
                "sage": [(1, sage_rows), (1, sage_degree_root), (2, lambda t, b: root("sage", t)),
                         (1, lambda t, b: copy_turned("sage", 4, t)), (3, sage_table), (1, sage_length),
                         (2, lambda t, b: copy_normed("sage", t))],
                "gcn1": [(1, lambda t, b: store("gcn1", "gcn2", t))],
                "gcn2": [(2, lambda t, b: root("gcn2", t)), (1, lambda t, b: copy_turned("gcn2", 1, t)),
                         (2, lambda t, b: store("gcn2", "hop1", t))],
                "hop1": [(1, lambda t, b: store("hop1", "hop2", t))],
                "hop2": [(1, lambda t, b: copy_turned("hop2", KB, t)), (2, lambda t, b: root("hop2", t)),
                         (4, lambda t, b: finish_relations("hop2", "rel1", t)),
                         (2, lambda t, b: copy_normed("hop2", t))],
                "rel1": [(1, lambda t, b: copy_turned("rel1", KB, t)),
                         (2, lambda t, b: finish_relations("rel1", "rel2", t))],
            }
            def ordered(n, names, order):
                named = dict(zip(names, (part for _, part in parts[n])))
                return [(back, named[what]) for back, what in order]

            ending = {
                "sage": ordered("sage", ("rows", "degree_root", "root", "copy_turned", "table", "length", "copy_normed"),
                                ((1, "rows"), (2, "root"), (1, "copy_turned"), (3, "table"), (1, "length"),
                                 (2, "copy_normed"), (1, "degree_root"), (1, "root"), (2, "table"),
                                 (1, "copy_normed"), (1, "table"))),
                "hop2": ordered("hop2", ("copy_turned", "root", "finish", "copy_normed"),
                                ((1, "copy_turned"), (2, "root"), (4, "finish"), (2, "copy_normed"), (3, "finish"),
                                 (1, "root"), (1, "copy_normed"), (2, "finish"), (1, "finish"))),
            }
            for n in NAMES[:-1]:
                over_tiles(act, None, parts[n], ending.get(n))
            with act.Fori(0, TILES - 1) as t:
                act.wait_ge(S["rel2", "table_ready"], t + 1)
                act.dma_start(out[bass.ds(t * P, P), :], xt(t)).then_inc(s_out, 16)
            act.wait_ge(S["rel2", "table_ready"], TILES)
            act.dma_start(out[(TILES - 1) * P:N, :], x_sb[0:LAST, (TILES - 1) * D:TILES * D]).then_inc(s_out, 16)

        @block.vector
        def _(dve):
            prep = Steps(dve, s_prep, 0, 0)

            def stats(k):
                lo, hi = NORMED[k]
                for t in range(lo, hi):
                    if t in dict(LOADED):
                        dve.wait_ge(s_x[[a for a, _ in LOADED].index(t)], 16)
                    nc.vector.bn_stats(bn_all[:, t, :], xt(t)).then_inc(s_bn, 1)
                dve.wait_ge(s_bn, hi)
                for t in range(lo, hi):
                    nc.vector.bn_aggr(mv_all[:, t, :], bn_all[:, t, :]).then_inc(s_mv, 1)

            def scales(k):
                lo, hi = NORMED[k]
                dve.wait_ge(s_std, k + 1)
                nc.vector.reciprocal(rstd_all[:, lo:hi], rstd_all[:, lo:hi]).then_inc(s_rstd, 1)
                dve.wait_ge(s_rstd, 2 * k + 1)
                nc.vector.scalar_tensor_tensor(shift_all[:, lo:hi], mv_all[:, lo:hi, 0], -1.0, rstd_all[:, lo:hi],
                                               ALU.mult, ALU.mult).then_inc(s_rstd, 1)

            for k in range(len(NORMED)):
                stats(k)
                if k < len(NORMED) - 1:
                    scales(k)

            dve.wait_ge(s_edge, 16 * 15)
            prep(nc.vector.tensor_tensor(drop, flat_i[:, F:2 * F], flat_next, ALU.is_gt))
            nc.vector.tensor_reduce(drops[0:QP, 0:1], drop, AXX, ALU.add).then_inc(s_drops, 1)
            scales(len(NORMED) - 1)
            for f, k in ((0, 0), (1, 1), (3, 2)):
                prep(nc.vector.tensor_copy(flat_f[:, f * F:(f + 1) * F], flat_i[:, k * F:(k + 1) * F]))
            nc.vector.tensor_copy(flat_f[:, 2 * F:3 * F], flat_w).then_inc(s_flat, 1)
            dve.wait_ge(s_dropmm, 1)
            nc.vector.tensor_copy(flag[:], prod2[:, 0:1]).then_inc(s_flag, 1)

            def copy_edges(first):
                for b in range(QB):
                    dve.wait_ge(s_flat_t, first + b + 1)
                    nc.vector.tensor_copy(
                        edges[:, b * QP:(b + 1) * QP, :],
                        y_ps[b % 2][:].rearrange("p a (g e) -> p e (a g)", g=2)[:, 0:QP, :]
                    ).then_inc(s_edgef, 1)
                dve.wait_ge(s_edgef, first + QB)

            copy_edges(0)

            dve.wait_ge(s_const, 5)

            def bucket_totals():
                prep = Steps(dve, s_sort_prep, 0, 0)
                prep(nc.vector.tensor_copy(tile_i, edges[:, :, 1]))
                prep(nc.vector.tensor_scalar(tile_i, tile_i, TSHIFT, None, ALU.logical_shift_right))
                prep(nc.vector.tensor_copy(tile_f, tile_i))
                prep(nc.vector.tensor_scalar(tile_f, tile_f, float(TILES), None, ALU.min))
                with dve.Fori(0, BUCKETS) as t:
                    step = Steps(dve, s_total_steps, 2, t)
                    step(nc.vector.tensor_scalar(mask, tile_f, iota[:, bass.ds(t, 1)], None, ALU.is_equal))
                    step(nc.vector.tensor_reduce(tot[:, bass.ds(t, 1)], mask, AXX, ALU.add))
                    step.close()

            def bucket_ends(prep, sums):
                prep(nc.vector.memset(ends[0][:, 0:32], 0.0))
                prep(nc.vector.memset(ends[1][:, 0:32], 0.0))
                prep(nc.vector.tensor_copy(ends[0][:, 32:], sums))
                for j in range(5):
                    a, b = ends[j % 2], ends[(j + 1) % 2]
                    prep(nc.vector.tensor_tensor(b[:, 32:], a[:, 32:], a[:, 32 - (1 << j):-(1 << j)], ALU.add))
                return ends[1][:, 32:]

            dve.wait_ge(s_flag, 1)
            with dve.If(out_of_order(dve) > 0):
                bucket_totals()
                dve.sem_inc(s_tot, 1)
                dve.wait_ge(s_totmm, 1)
                sort = Steps(dve, s_sort, 0, 0)
                end = bucket_ends(sort, prod[:, 0:BUCKETS])
                sort(nc.vector.tensor_copy(totals, prod[:, 0:BUCKETS]))
                sort(nc.vector.tensor_tensor(base, end, totals, ALU.subtract))
                sort(nc.vector.scalar_tensor_tensor(base, base, -1.0, prod[:, 64:64 + BUCKETS], ALU.add, ALU.add))
                sort(nc.vector.memset(scan[0][:, 0:256], 0.0))
                sort(nc.vector.memset(scan[1][:, 0:256], 0.0))
                sort(nc.vector.memset(pos, 0.0))
                with dve.Fori(0, BUCKETS) as t:
                    step = Steps(dve, s_rank, 13, t)
                    step(nc.vector.tensor_scalar(scan[0][:, 256:], tile_f, iota[:, bass.ds(t, 1)], None, ALU.is_equal))
                    step(nc.vector.tensor_copy(mask, scan[0][:, 256:]))
                    for j in range(9):
                        a, b = scan[j % 2], scan[(j + 1) % 2]
                        step(nc.vector.tensor_tensor(b[:, 256:], a[:, 256:], a[:, 256 - (1 << j):-(1 << j)], ALU.add))
                    step(nc.vector.scalar_tensor_tensor(mask, scan[1][:, 256:], base[:, bass.ds(t, 1)], mask,
                                                        ALU.add, ALU.mult))
                    step(nc.vector.tensor_tensor(pos, pos, mask, ALU.add))
                    step.close()
                sort(nc.vector.tensor_copy(pos_u, pos))
                dve.sem_inc(s_pos, 1)
                copy_edges(QB)

            nc.vector.tensor_copy(idx_node[:], edges[:, :, 0]).then_inc(s_idx, 1)
            nc.vector.scalar_tensor_tensor(idx_rel[:], edges[:, :, 3], float(NPAD), edges[:, :, 0],
                                           ALU.mult, ALU.add).then_inc(s_idx, 1)
            near = slice(BOUNDS - 31, P)
            group_ends = edges[:].rearrange("p (q k) f -> p q k f", k=QUAD)[near, :, QUAD - 1, 1]
            tile_ends = iota[:].rearrange("p (t i) -> p t i", i=P)[near, :, P - 1]
            prep(nc.vector.tensor_tensor(within[near], tile_ends.unsqueeze(2).broadcast_to([32, TILES, QUADS]),
                                         group_ends.unsqueeze(1).broadcast_to([32, TILES, QUADS]), ALU.is_ge))
            prep(nc.vector.tensor_reduce(groups[near], within[near], AXX, ALU.add))
            prep(nc.vector.memset(bounds[near], 0))
            prep(nc.vector.tensor_copy(bounds[near, 1:], groups[near]))
            dve.sem_inc(s_bounds, 1)

            nc.vector.memset(one_w[:, :, 0], 1.0).then_inc(s_idx, 1)
            prep(nc.vector.tensor_copy(one_w[:, :, 1], edges[:, :, 2]))
            prep(nc.vector.tensor_tensor(rest_w, edges[:, :, 2], one_w[:, :, 1], ALU.subtract))
            prep(nc.vector.tensor_copy(one_w[:, :, 2], rest_w))
            prep(nc.vector.tensor_tensor(rest_w2, rest_w, one_w[:, :, 2], ALU.subtract))
            prep(nc.vector.tensor_copy(one_w[:, :, 3], rest_w2))
            dve.sem_inc(s_weights, 1)
            dve.wait_ge(s_wtc, 3)

            def norm(n, step, rows, to):
                dve.sem_inc(s_passed[1], 1)
                step(nc.vector.bn_stats(bnst[:], rows))
                dve.sem_inc(s_passed[1], 1)
                nc.vector.bn_aggr(small[:, 0, 0:2], bnst[:]).then_inc(S[n, "var_ready"], 1)
                dve.wait_ge(S[n, "std_ready"], step.t + 1)
                step(nc.vector.reciprocal(small[:, 0, 3:4], small[:, 0, 2:3]))
                step(nc.vector.tensor_scalar(post2n[:], rows, small[:, 0, 0:1], 0.0, ALU.subtract, ALU.max))
                step(nc.vector.tensor_scalar(to, post2n[:], small[:, 0, 3:4], None, ALU.mult))

            def visits_of(n):
                weighted = PASSES[n][0]
                free0 = before(n) * 2 * VISITS

                def group(q, t, half, first=False):
                    u = q + t
                    places = iota[:, bass.ds(t * P, P)]
                    for k in range(0, QUAD, 2):
                        dve.wait_ge(pair_free, u * 2 + (free0 + k // 2 + (3 if first else 1)))
                        at = half * QUAD + k
                        pair = edges[:, bass.ds(q * QUAD + k, 2), :]
                        if n == "sage" or not weighted:
                            ins = nc.vector.tensor_tensor((onehot1 if n == "sage" else onehot)[:, at:at + 2, :],
                                                          places.unsqueeze(1).broadcast_to([P, 2, P]),
                                                          pair[:, :, 1:2].broadcast_to([P, 2, P]), ALU.is_equal)
                        if weighted:
                            for j in range(2):
                                edge = pair[:, j:j + 1, :].rearrange("p c f -> p (c f)")
                                ins = nc.vector.tensor_scalar(onehot[:, at + j, :], places, edge[:, 1:2], edge[:, 2:3],
                                                              ALU.is_equal, ALU.mult)
                        ins.then_inc(onehot_ready, 1)

                def visits(t, b, limits):
                    lo, hi = limits
                    over_groups(dve, lo, hi, lambda q, half, first=False: group(q, t, half, first))
                return visits

            def d(t, k):
                return dinv[:, bass.ds(t, 1), k:k + 1].rearrange("p a b -> p (a b)")

            def half_d(t):
                return hdinv[:, bass.ds(t, 1)]

            def rows_free(n, t):
                dve.wait_ge(S[n, "rows_turned"], t + 1)

            def normed_free(n, t):
                dve.wait_ge(S[n, "normed_turned"], t + 1)

            def relations(n, t):
                rows, shared = relation_rows(n, t)
                for g in range(REL // 2):
                    if shared:
                        dve.wait_ge(pair_stored[g], t * 16 + (16 * TILES * (n == "rel1") + 1))
                    dve.wait_ge(S[n, "y_ready"], t * (REL // 2) + (g + 1))
                    nc.vector.tensor_tensor(rows[:, 2 * g:2 * g + 2, :], y_ps[g][:], relb_sb[:], ALU.add
                                            ).then_inc(S[n, "y_added"], 1)

            def sage_degrees(t, b):
                n = "sage"
                step = Steps(dve, S[n, "dve_steps"], 4, t)
                dve.wait_ge(S[n, "rows_ready"], t + 1)
                step(nc.vector.tensor_copy(small[:, b, 12:13], post[:, D:D + 1]))
                step(nc.vector.tensor_reduce(small[:, b, 13:14], post[:, D + 1:D + 4], AXX, ALU.add))
                step(nc.vector.tensor_scalar(small[:, b, 6:8], small[:, b, 12:14], 1.0, None, ALU.add))
                step(nc.vector.tensor_scalar(small[:, b, 8:10], small[:, b, 6:8], DEG_EPS, None, ALU.max))
                dve.sem_inc(S[n, "degree_ready"], 1)
                step.close()

            def sage_product(t, b):
                n = "sage"
                step = Steps(dve, S[n, "dve_steps2"], 10, t)
                dve.wait_ge(S[n, "degree_root"], t + 1)
                step(nc.vector.reciprocal(small[:, b, 12:14], small[:, b, 10:12]))
                dt_ = dinv[:, bass.ds(t, 1), :].rearrange("p a b -> p (a b)")
                step(nc.vector.scalar_tensor_tensor(dt_, small[:, b, 6:8], 0.0, small[:, b, 12:14], ALU.is_gt, ALU.mult))
                step(nc.vector.tensor_scalar(half_d(t), d(t, 1), 0.5, None, ALU.mult))
                dve.wait_ge(S[n, "length_ready"], t + 1)
                step(nc.vector.tensor_scalar(small[:, b, 14:15], small[:, b, 5:6], NORM_EPS, None, ALU.max))
                step(nc.vector.reciprocal(small[:, b, 15:16], small[:, b, 14:15]))
                step(nc.vector.scalar_tensor_tensor(xt(t), prod[:, 0:D], small[:, b, 15:16], xt(t), ALU.mult, ALU.add))
                dve.sem_inc(S[n, "product_free"], 1)
                normed_free(n, t)
                norm(n, step, xt(t), normed[:, b, :])
                dve.sem_inc(S[n, "normed_ready"], 1)
                step.close()

            def gcn1_rows(t, b):
                n = "gcn1"
                step = Steps(dve, S[n, "dve_steps"], 4, t)
                dve.wait_ge(agg_ready, t + (before(n) * TILES + 1))
                step(nc.vector.tensor_tensor(post[:, 0:HID], agg[b][:, 0:HID], tt(t, HID), ALU.add))
                dve.sem_inc(agg_free, 1)
                step(nc.vector.tensor_scalar(post[:, 0:HID], post[:, 0:HID], d(t, 0), None, ALU.mult))
                step(nc.vector.tensor_tensor(post[:, 0:HID], post[:, 0:HID], b1_sb[:], ALU.add))
                step(nc.vector.tensor_scalar(tt(t, HID), post[:, 0:HID], 0.0, d(t, 0), ALU.max, ALU.mult))
                dve.sem_inc(S[n, "table_ready"], 1)
                step.close()

            def gcn2_rows(t, b):
                n = "gcn2"
                step = Steps(dve, S[n, "dve_steps"], 2, t)
                dve.wait_ge(agg_ready, t + (before(n) * TILES + 1))
                rows_free(n, t)
                step(nc.vector.tensor_tensor(post[:, 0:HID], agg[b][:, 0:HID], tt(t, HID), ALU.add))
                dve.sem_inc(agg_free, 1)
                step(nc.vector.tensor_scalar(post[:, 0:HID], post[:, 0:HID], d(t, 0), None, ALU.mult))
                dve.sem_inc(S[n, "rows_ready"], 1)
                step.close()

            def gcn2_product(t, b):
                n = "gcn2"
                step = Steps(dve, S[n, "dve_steps2"], 7, t)
                step(nc.vector.tensor_tensor(xt(t), xt(t), b2_sb[:], ALU.add))
                dve.wait_ge(S[n, "product_ready"], t + 1)
                step(nc.vector.tensor_tensor(xt(t), prod[:, 0:D], xt(t), ALU.add))
                dve.sem_inc(S[n, "product_free"], 1)
                norm(n, step, xt(t), ht(t))
                step(nc.vector.tensor_scalar(tt(t), ht(t), d(t, 1), None, ALU.mult))
                dve.sem_inc(S[n, "table_ready"], 1)
                step.close()

            def hop(step, n, t, b):
                dve.wait_ge(agg_ready, t + (before(n) * TILES + 1))
                if n == "hop2":
                    rows_free(n, t)
                step(nc.vector.tensor_tensor(post[:, 0:D], agg[b][:, 0:D], tt(t), ALU.add))
                dve.sem_inc(agg_free, 1)
                if n == "hop1":
                    step(nc.vector.tensor_scalar(ht(t), ht(t), 0.5, None, ALU.mult))
                step(nc.vector.scalar_tensor_tensor(post[:, 0:D], post[:, 0:D], half_d(t), ht(t), ALU.mult, ALU.add))

            def hop1_rows(t, b):
                step = Steps(dve, S["hop1", "dve_steps"], 4, t)
                hop(step, "hop1", t, b)
                step(nc.vector.tensor_scalar(tt(t), post[:, 0:D], d(t, 1), None, ALU.mult))
                dve.sem_inc(S["hop1", "table_ready"], 1)
                step.close()

            def hop2_rows(t, b):
                n = "hop2"
                step = Steps(dve, S[n, "dve_steps"], 3, t)
                hop(step, n, t, b)
                step(nc.vector.tensor_scalar(post[:, 0:D], post[:, 0:D], 0.0, None, ALU.max))
                dve.sem_inc(S[n, "rows_ready"], 1)
                step.close()

            def hop2_product(t, b):
                n = "hop2"
                step = Steps(dve, S[n, "dve_steps2"], 6, t)
                step(nc.vector.tensor_tensor(xt(t), xt(t), hopb_sb[:], ALU.add))
                dve.wait_ge(S[n, "product_ready"], t + 1)
                step(nc.vector.tensor_tensor(xt(t), prod[:, 0:D], xt(t), ALU.add))
                dve.sem_inc(S[n, "product_free"], 1)
                normed_free(n, t)
                norm(n, step, xt(t), normed[:, b, :])
                dve.sem_inc(S[n, "normed_ready"], 1)
                step.close()

            def rel1_rows(t, b):
                n = "rel1"
                step = Steps(dve, S[n, "dve_steps"], 1, t)
                dve.wait_ge(agg_ready, t + (before(n) * TILES + 1))
                rows_free(n, t)
                step(nc.vector.tensor_copy(post[:, 0:D], agg[b][:, 0:D]))
                dve.sem_inc(agg_free, 1)
                dve.sem_inc(S[n, "rows_ready"], 1)
                step.close()

            def rel2_rows(t, b):
                n = "rel2"
                step = Steps(dve, S[n, "dve_steps"], 1, t)
                dve.wait_ge(agg_ready, t + (before(n) * TILES + 1))
                step(nc.vector.tensor_tensor(xt(t), agg[b][:, 0:D], xt(t), ALU.add))
                dve.sem_inc(agg_free, 1)
                dve.sem_inc(S[n, "table_ready"], 1)
                step.close()

            parts = {
                "sage": [(1, sage_degrees), (2, sage_product)],
                "gcn1": [(1, gcn1_rows)],
                "gcn2": [(2, gcn2_product), (1, gcn2_rows)],
                "hop1": [(1, hop1_rows)],
                "hop2": [(1, hop2_rows), (4, lambda t, b: relations("hop2", t)), (2, hop2_product)],
                "rel1": [(1, rel1_rows), (2, lambda t, b: relations("rel1", t))],
                "rel2": [(1, rel2_rows)],
            }
            rel = parts["hop2"][1][1]
            ending = {"sage": [(2, sage_product), (1, sage_degrees), (1, sage_product)],
                      "gcn2": [(1, gcn2_rows), (2, gcn2_product), (1, gcn2_product)],
                      "hop2": [(1, hop2_rows), (4, rel), (2, hop2_product), (3, rel), (1, hop2_product), (2, rel),
                               (1, rel)]}
            for n in NAMES:
                if n in ("hop2", "rel1"):
                    dve.wait_ge(s_wrel[0 if n == "hop2" else 1], 16 * (KB + 2))
                over_tiles(dve, visits_of(n), parts[n], ending.get(n), early=n == "sage")


_INS = ["x", "src", "dst", "edge_type_8", "edge_weight", "L0_gnn_w_self", "L0_gnn_w_neigh", "L1_gnn_W1",
        "L1_gnn_b1", "L1_gnn_W2", "L1_gnn_b2", "L2_gnn_W", "L2_gnn_b", "L3_gnn_W0", "L3_gnn_b0",
        "L3_gnn_W1", "L3_gnn_b1"]


def kernel(**inputs):
    import concourse.bacc as bacc
    from concourse.bass_utils import run_bass_kernel_spmd

    nc = bacc.Bacc("TRN2", target_bir_lowering=False, num_devices=1)
    arrays, args = {}, []
    for name in _INS:
        a = np.ascontiguousarray(inputs[name])
        arrays[f"in_{name}"] = a
        args.append(nc.dram_tensor(f"in_{name}", a.shape, mybir.dt.from_np(a.dtype), kind="ExternalInput").ap())
    shape = inputs["x"].shape
    args.append(nc.dram_tensor("out_x", shape, F32, kind="ExternalOutput").ap())
    build_gnn(nc, *args)
    result = run_bass_kernel_spmd(nc, [arrays], core_ids=[0])
    return result.results[0]["out_x"]
```
